# Optimizing a Trainium2 kernel written in Bass

```python
import numpy as np
import jax
import jax.numpy as jnp

def _softmax(x, axis=-1):
    return jax.nn.softmax(x, axis=axis)

def _gelu(x):
    return jax.nn.gelu(x, approximate=True)

def _silu(x):
    return jax.nn.silu(x)

def _sigmoid(x):
    return jax.nn.sigmoid(x)

def _layernorm(x, axis=-1, eps=1e-05):
    m = jnp.mean(x, axis=axis, keepdims=True)
    v = jnp.var(x, axis=axis, keepdims=True)
    return (x - m) / jnp.sqrt(v + eps)

def _scatter_add(tgt, idx, src, axis=0):
    return tgt.at[idx].add(src)

def _segment_sum(src, seg, n):
    return jax.ops.segment_sum(src, seg, n)
kernel_name = 'mk_seq_postln_d2_jaxref_r8_b075c5'

def setup_inputs(seed: int=0):
    np.random.seed(seed)
    _w = jnp.asarray

    def _L0_attn_setup():
        import jax, jax.numpy as jnp
        import numpy as np
        import math
        D_MODEL = 256
        NUM_HEAD = 16
        HEAD_DIM = D_MODEL // NUM_HEAD

        def _trunc_normal(key, shape, std):
            return jax.random.truncated_normal(key, -3.0, 3.0, shape, dtype=jnp.float32) * std
        key = jax.random.key(seed)
        kx, kp, ko = jax.random.split(key, 3)
        b, s = (4, 256)
        x = jax.random.normal(kx, (b, s, D_MODEL), dtype=jnp.float32)
        sigma_p = math.sqrt(2.0 / (D_MODEL + 3 * D_MODEL))
        w_project = _trunc_normal(kp, (3 * D_MODEL, D_MODEL), sigma_p)
        sigma_o = math.sqrt(2.0 / (D_MODEL + D_MODEL))
        w_out = _trunc_normal(ko, (D_MODEL, D_MODEL), sigma_o)
        return {'x': x, 'w_project': w_project, 'w_out': w_out}
    _L0_attn_in = _L0_attn_setup()

    def _L0_ffn_setup():
        import jax, jax.numpy as jnp
        import numpy as np
        HIDDEN = 256
        INTER = 704
        B, S = (2, 256)

        def _ternary(key, shape):
            return jax.random.randint(key, shape, -1, 2).astype(jnp.float32)
        key = jax.random.key(seed)
        ks = jax.random.split(key, 7)
        x = jax.random.normal(ks[0], (B, S, HIDDEN), dtype=jnp.float32)
        gate_w = _ternary(ks[1], (INTER, HIDDEN))
        up_w = _ternary(ks[2], (INTER, HIDDEN))
        down_w = _ternary(ks[3], (HIDDEN, INTER))
        gate_s = jax.random.uniform(ks[4], (INTER,), minval=0.01, maxval=0.1, dtype=jnp.float32)
        up_s = jax.random.uniform(ks[5], (INTER,), minval=0.01, maxval=0.1, dtype=jnp.float32)
        down_s = jax.random.uniform(ks[6], (HIDDEN,), minval=0.01, maxval=0.1, dtype=jnp.float32)
        return {'x': x, 'gate_w': gate_w, 'up_w': up_w, 'down_w': down_w, 'gate_s': gate_s, 'up_s': up_s, 'down_s': down_s}
    _L0_ffn_in = _L0_ffn_setup()

    def _L1_attn_setup():
        import jax, jax.numpy as jnp
        import numpy as np
        HIDDEN = 256
        HEADS = 16
        HEAD_DIM = HIDDEN // HEADS
        key = jax.random.key(seed)
        ks = jax.random.split(key, 9)
        B, S = (2, 256)
        x = jax.random.normal(ks[0], (B, S, HIDDEN), dtype=jnp.float32)
        scale = 1.0 / np.sqrt(HIDDEN)
        Wq = jax.random.normal(ks[1], (HIDDEN, HIDDEN), dtype=jnp.float32) * scale
        Wk = jax.random.normal(ks[2], (HIDDEN, HIDDEN), dtype=jnp.float32) * scale
        Wv = jax.random.normal(ks[3], (HIDDEN, HIDDEN), dtype=jnp.float32) * scale
        Wo = jax.random.normal(ks[4], (HIDDEN, HIDDEN), dtype=jnp.float32) * scale
        bq = jnp.zeros((HIDDEN,), dtype=jnp.float32)
        bk = jnp.zeros((HIDDEN,), dtype=jnp.float32)
        bv = jnp.zeros((HIDDEN,), dtype=jnp.float32)
        bo = jnp.zeros((HIDDEN,), dtype=jnp.float32)
        return {'x': x, 'Wq': Wq, 'bq': bq, 'Wk': Wk, 'bk': bk, 'Wv': Wv, 'bv': bv, 'Wo': Wo, 'bo': bo}
    _L1_attn_in = _L1_attn_setup()

    def _L1_ffn_setup():
        import jax, jax.numpy as jnp
        import numpy as np
        D_MODEL = 256
        D_EXPERT = 1024
        EPS = 1e-08

        def ternary_quant(w):
            scale = jnp.mean(jnp.abs(w)) + EPS
            q = jnp.clip(jnp.round(w / scale), -1.0, 1.0) * scale
            return w + jax.lax.stop_gradient(q - w)
        key = jax.random.key(seed)
        k_x, k_up, k_gate, k_down = jax.random.split(key, 4)
        std_in = 1.0 / np.sqrt(D_MODEL)
        std_exp = 1.0 / np.sqrt(D_EXPERT)
        return {'x': jax.random.normal(k_x, (4, 256, D_MODEL), dtype=jnp.float32), 'W_up': jax.random.normal(k_up, (D_EXPERT, D_MODEL), dtype=jnp.float32) * std_in, 'W_gate': jax.random.normal(k_gate, (D_EXPERT, D_MODEL), dtype=jnp.float32) * std_in, 'W_down': jax.random.normal(k_down, (D_MODEL, D_EXPERT), dtype=jnp.float32) * std_exp}
    _L1_ffn_in = _L1_ffn_setup()
    _d = {'L0_attn_x': _L0_attn_in['x'], 'L0_attn_w_project': _L0_attn_in['w_project'], 'L0_attn_w_out': _L0_attn_in['w_out'], 'L0_ffn_gate_w': _L0_ffn_in['gate_w'], 'L0_ffn_up_w': _L0_ffn_in['up_w'], 'L0_ffn_down_w': _L0_ffn_in['down_w'], 'L0_ffn_gate_s': _L0_ffn_in['gate_s'], 'L0_ffn_up_s': _L0_ffn_in['up_s'], 'L0_ffn_down_s': _L0_ffn_in['down_s'], 'L1_attn_Wq': _L1_attn_in['Wq'], 'L1_attn_bq': _L1_attn_in['bq'], 'L1_attn_Wk': _L1_attn_in['Wk'], 'L1_attn_bk': _L1_attn_in['bk'], 'L1_attn_Wv': _L1_attn_in['Wv'], 'L1_attn_bv': _L1_attn_in['bv'], 'L1_attn_Wo': _L1_attn_in['Wo'], 'L1_attn_bo': _L1_attn_in['bo'], 'L1_ffn_W_up': _L1_ffn_in['W_up'], 'L1_ffn_W_gate': _L1_ffn_in['W_gate'], 'L1_ffn_W_down': _L1_ffn_in['W_down']}
    _x0 = _d['L0_attn_x']
    _d['L0_attn_x'] = jax.random.normal(jax.random.fold_in(jax.random.key(seed), 1), (4, 256, 256), dtype=_x0.dtype)
    del _x0
    return _d

def reference(L0_attn_x, L0_attn_w_project, L0_attn_w_out, L0_ffn_gate_w, L0_ffn_up_w, L0_ffn_down_w, L0_ffn_gate_s, L0_ffn_up_s, L0_ffn_down_s, L1_attn_Wq, L1_attn_bq, L1_attn_Wk, L1_attn_bk, L1_attn_Wv, L1_attn_bv, L1_attn_Wo, L1_attn_bo, L1_ffn_W_up, L1_ffn_W_gate, L1_ffn_W_down):

    def _L0_attn_ref(x, w_project, w_out):
        import jax, jax.numpy as jnp
        import numpy as np
        import math
        D_MODEL = 256
        NUM_HEAD = 16
        HEAD_DIM = D_MODEL // NUM_HEAD

        def _trunc_normal(key, shape, std):
            return jax.random.truncated_normal(key, -3.0, 3.0, shape, dtype=jnp.float32) * std
        b, s, d = x.shape
        qkv = jnp.einsum('bsd,od->bso', x, w_project)
        qkv = qkv.reshape(b, s, 3, NUM_HEAD, HEAD_DIM)
        qkv = jnp.transpose(qkv, (2, 0, 3, 1, 4))
        q, k, v = (qkv[0], qkv[1], qkv[2])
        att = jnp.einsum('bhqd,bhkd->bhqk', q, k) / math.sqrt(HEAD_DIM)
        causal = jnp.triu(jnp.ones((s, s), dtype=bool), k=1)
        att = jnp.where(causal[None, None, :, :], jnp.float32(-1000000000.0), att)
        att = jax.nn.softmax(att, axis=-1)
        out = jnp.einsum('bhqk,bhkd->bhqd', att, v)
        out = jnp.transpose(out, (0, 2, 1, 3)).reshape(b, s, d)
        return jnp.einsum('bsd,od->bso', out, w_out)

    def _L0_ffn_ref(x, gate_w, up_w, down_w, gate_s, up_s, down_s):
        import jax, jax.numpy as jnp
        import numpy as np
        HIDDEN = 256
        INTER = 704
        B, S = (2, 256)

        def _ternary(key, shape):
            return jax.random.randint(key, shape, -1, 2).astype(jnp.float32)
        b, s, h = x.shape
        xf = x.reshape(b * s, h)
        g = jnp.einsum('th,ih->ti', xf, gate_w) * gate_s
        u = jnp.einsum('th,ih->ti', xf, up_w) * up_s
        hdn = jax.nn.silu(g) * u
        out = jnp.einsum('ti,hi->th', hdn, down_w) * down_s
        return out.reshape(b, s, -1)

    def _L1_attn_ref(x, Wq, bq, Wk, bk, Wv, bv, Wo, bo):
        import jax, jax.numpy as jnp
        import numpy as np
        HIDDEN = 256
        HEADS = 16
        HEAD_DIM = HIDDEN // HEADS
        B, S, H = x.shape
        nh, hd = (HEADS, HEAD_DIM)
        q = (x @ Wq.T + bq).reshape(B, S, nh, hd).transpose(0, 2, 1, 3)
        k = (x @ Wk.T + bk).reshape(B, S, nh, hd).transpose(0, 2, 1, 3)
        v = (x @ Wv.T + bv).reshape(B, S, nh, hd).transpose(0, 2, 1, 3)
        scores = jnp.einsum('bhqd,bhkd->bhqk', q, k) / np.sqrt(hd)
        causal = jnp.tril(jnp.ones((S, S), dtype=bool))
        scores = jnp.where(causal[None, None], scores, -jnp.inf)
        probs = jax.nn.softmax(scores, axis=-1)
        attn = jnp.einsum('bhqk,bhkd->bhqd', probs, v)
        y = attn.transpose(0, 2, 1, 3).reshape(B, S, H)
        return y @ Wo.T + bo

    def _L1_ffn_ref(x, W_up, W_gate, W_down):
        import jax, jax.numpy as jnp
        import numpy as np
        D_MODEL = 256
        D_EXPERT = 1024
        EPS = 1e-08

        def ternary_quant(w):
            scale = jnp.mean(jnp.abs(w)) + EPS
            q = jnp.clip(jnp.round(w / scale), -1.0, 1.0) * scale
            return w + jax.lax.stop_gradient(q - w)
        wu = ternary_quant(W_up)
        wg = ternary_quant(W_gate)
        wd = ternary_quant(W_down)
        up = jnp.einsum('bsd,ed->bse', x, wu)
        gate = jnp.einsum('bsd,ed->bse', x, wg)
        hidden = jax.nn.silu(up) * gate
        return jnp.einsum('bse,de->bsd', hidden, wd)
    x = L0_attn_x
    x = _layernorm(x + _L0_attn_ref(x, L0_attn_w_project, L0_attn_w_out), axis=-1)
    x = _layernorm(x + _L0_ffn_ref(x, L0_ffn_gate_w, L0_ffn_up_w, L0_ffn_down_w, L0_ffn_gate_s, L0_ffn_up_s, L0_ffn_down_s), axis=-1)
    x = _layernorm(x + _L1_attn_ref(x, L1_attn_Wq, L1_attn_bq, L1_attn_Wk, L1_attn_bk, L1_attn_Wv, L1_attn_bv, L1_attn_Wo, L1_attn_bo), axis=-1)
    x = _layernorm(x + _L1_ffn_ref(x, L1_ffn_W_up, L1_ffn_W_gate, L1_ffn_W_down), axis=-1)
    return x

_drawn_inputs = setup_inputs


def setup_inputs(seed=0):
    import zlib

    import numpy as np

    out = dict(_drawn_inputs(seed))
    spreads = {'L1_attn_bq': (0.0, 0.418),
     'L1_attn_bk': (0.0, 0.8),
     'L1_attn_bv': (0.0, 0.1),
     'L1_attn_bo': (0.0, 0.1)}
    factors = {}
    for name, (base, spread) in spreads.items():
        noise = np.random.default_rng([zlib.crc32(name.encode()), seed]).standard_normal(out[name].shape)
        drawn = base * np.exp(spread * noise) if base else spread * noise
        out[name] = jnp.asarray(drawn.astype(out[name].dtype))
    for name, factor in factors.items():
        out[name] = (out[name] * factor).astype(out[name].dtype)
    return out
```

```python
from contextlib import ExitStack

import concourse.bass as bass
from concourse import mybir

fp32 = mybir.dt.float32
f32r = mybir.dt.float32r
bf16 = mybir.dt.bfloat16
ALU = mybir.AluOpType
ACT = mybir.ActivationFunctionType

NB, T, D = 4, 256, 256
H, HD = 16, 16
NS = 8
P = 128
KT = D // P
TT = T // P
INTER = 704
MT0 = -(-INTER // P)
EXPERT = 1024
MT1 = EXPERT // P
EPS = 1e-5
QEPS = 1e-8
SC = 1.0 / HD ** 0.5
NEG = -3.0e38
NGI = 4


PREP0 = 7
PREP1 = 4
TERN = 6


def schedule():
    o = []

    def put(step, l=0, b=0, i=0):
        o.append((step, l, b, i))

    def attention(l, todo, before):
        put("QK", l, 0); put("V", l, 0)
        before(0)
        put("QK", l, 1); put("V", l, 1)
        for s in range(NS):
            put("S", l, 0, s)
        before(1)
        put("MX", l, 0)
        for b in range(NB):
            for s in range(NS):
                if b + 1 < NB:
                    put("S", l, b + 1, s)
                put("ST", l, b, s)
                if todo:
                    step = todo.pop(0)
                    if step:
                        put(*step)
                if s >= 2 and s % 2 == 0:
                    put("PV", l, b, s // 2 - 1)
                if b > 0:
                    if s == 0: put("UT", l, b - 1)
                    if s == 1: put("YT", l, b - 1)
                    if s == 2: put("O", l, b - 1)
                    if s == 3: put("LN", 2 * l, b - 1)
                    if s == 5: put("XT", 2 * l, b - 1)
                if b + 2 < NB and s == 3: put("QK", l, b + 2)
            if b + 1 < NB: put("MX", l, b + 1)
            if b + 2 < NB: put("V", l, b + 2)
            put("PV", l, b, NGI - 1)
        for step in todo:
            if step:
                put(*step)
        put("UT", l, NB - 1)

    def ffn(l):
        for b in range(NB):
            for mp in range((MT0, MT1)[l] // 2):
                put("GU", l, b, mp)
                if b == 0 and mp == 0: put("YT", l, NB - 1)
                if b == 0 and mp == 1: put("O", l, NB - 1); put("LN", 2 * l, NB - 1)
                if b == 1 and mp == 0: put("XT", 2 * l, NB - 1)
                if b > 0 and mp == 1: put("D", l, b - 1); put("LN", 2 * l + 1, b - 1)
                if b > 1 and mp == 0 and l == 0: put("XT", 1, b - 2)
                if l == 0 and b == 1:
                    put("PREP1", 0, 0, mp)
            if l == 0 and b == 1:
                put("PREP1", 0, 0, 3)

    def last_ffn(i):
        if i == 0:
            put("D", 0, NB - 1); put("XT", 1, NB - 2); put("LN", 1, NB - 1)
        if i == 1:
            put("XT", 1, NB - 1)

    tern = []
    for m in range(3):
        tern += [("TERN", 1, 0, TERN * m + r) for r in range(TERN)] + [None] * 4
    put("PREPA")
    attention(0, [("PREP0", 0, 0, k) for k in range(PREP0)], lambda i: None)
    ffn(0)
    attention(1, tern, last_ffn)
    ffn(1)
    put("D", 1, NB - 1); put("LN", 3, NB - 1)
    return o


def program(nc, x_nat, x_tr, a0, f0gu, f0dn, gs, us, ds_row, a1, bqk, brow, f1, out):
    order = schedule()

    count, seen = {}, {}
    for step in order:
        seen[step[0]] = seen.get(step[0], 0) + 1
        count[step] = seen[step[0]]

    def nth(step, l=0, b=0, i=0):
        return count[(step, l, b, i)]

    st_steps = [q for q in order if q[0] == "ST"]
    assert [(2 * q[1] + (q[0] == "D"), q[2]) for q in order if q[0] in "OD"] == [q[1:3] for q in order if q[0] == "LN"]

    def ln_of(step, l, b):
        return nth("LN", 2 * l + (step == "D"), b)

    batches = [(l, b) for l in range(2) for b in range(NB)]

    def users(l, b):
        return [q for q in batches if q < (l, b) and q[1] % 3 == b % 3]

    ctx = ExitStack()
    with ctx:
        def sb(name, shape, dt=fp32):
            return ctx.enter_context(nc.sbuf_tensor(name, shape, dt))

        def sem(name):
            return ctx.enter_context(nc.semaphore(name))

        x = sb("x", [P, NB * TT, D])
        xT_hi = sb("xT_hi", [P, KT, NB * T], f32r)
        xT_lo = sb("xT_lo", [P, KT, NB * T], f32r)
        ident = sb("ident", [P, P])
        mask = sb("mask", [P, 384])
        ones = sb("ones", [P, P])
        ones_row = sb("ones_row", [1, P], f32r)
        raw = sb("raw", [P, 2048])
        wa_hi = sb("wa_hi", [P, KT, 4 * D], f32r)
        wa_lo = sb("wa_lo", [P, KT, 4 * D], f32r)
        gu_hi = sb("gu_hi", [P, KT * 2 * MT0 * P], f32r)
        gu_lo = sb("gu_lo", [P, KT * 2 * MT0 * P], f32r)
        dn = sb("dn", [P, 2 * MT0 * D], f32r)
        qk_bias = sb("qk_bias", [P, 4])
        b_hi = sb("b_hi", [1, 2 * D], f32r)
        b_lo = sb("b_lo", [1, 2 * D], f32r)
        gs_c = sb("gs_c", [P, MT0])
        us_c = sb("us_c", [P, MT0])
        half_gs = sb("half_gs", [P, MT0])
        gain = sb("gain", [P, MT0])
        ds_b = sb("ds_b", [P, D])
        q_hi = sb("q_hi", [P, 2, T], f32r)
        q_lo = sb("q_lo", [P, 2, T], f32r)
        k_hi = sb("k_hi", [P, 2, T], f32r)
        k_lo = sb("k_lo", [P, 2, T], f32r)
        q_stack = [sb(f"q_stack{n}", [P, NS, T], f32r) for n in range(3)]
        k_stack = [sb(f"k_stack{n}", [P, NS, T], f32r) for n in range(3)]
        v_aug = [sb(f"v_aug{n}", [P, TT, H, 2 * HD]) for n in range(3)]
        masked = sb("masked", [P, 2, T + P], bf16)
        row_max = sb("row_max", [P, 2, H])
        max_hl = sb("max_hl", [P, 2, P])
        maxT = sb("maxT", [2 * H, T], f32r)
        probs_all = sb("probs", [P, 4 * 2 * (T + P)])
        probs = [probs_all[:, n * 2 * (T + P):(n + 1) * 2 * (T + P)].rearrange("p (j t) -> p j t", j=2) for n in range(4)]
        xT_raw = probs_all[:, 0:KT * NB * T].rearrange("p (k t) -> p k t", k=KT)
        u_sb = sb("u_sb", [P, NGI, T])
        den_inv = sb("den_inv", [P, 2, H])
        y = sb("y", [P, TT, D])
        yT_hi = sb("yT_hi", [P, KT, T], f32r)
        yT_lo = sb("yT_lo", [P, KT, T], f32r)
        res = [sb(f"res{n}", [P, TT, D]) for n in range(2)]
        stats = [sb(f"stats{n}", [P, TT, 6]) for n in range(2)]
        mv = [sb(f"mv{n}", [P, TT, 2]) for n in range(2)]
        rstd = [sb(f"rstd{n}", [P, TT]) for n in range(2)]
        minus_half = sb("minus_half", [P, TT])
        th = [sb(f"th{n}", [P, 512]) for n in range(2)]
        hf = [sb(f"hf{n}", [P, 512]) for n in range(2)]
        piece, junk, b_row = hf, th, th[1][0:1, :]
        hidden1_lo = sb("hidden1_lo", [P, MT1, T], f32r)
        hidden = [(q_stack[0], q_stack[1]), (q_stack[2], hidden1_lo)]
        abs_sum = sb("abs_sum", [P, 3, 4])
        scale = sb("scale", [P, 3])
        half = sb("half", [P, 3])
        minus = sb("minus", [P, 3])
        total = sb("total", [P, 3])
        out_gain = sb("out_gain", [P, 1])

        bank = {n: ctx.enter_context(nc.psum_tensor(f"bank{n}", [P, 512], fp32)) for n in (0, 1)}
        pairs = [ctx.enter_context(nc.psum_tensor(f"pair{n}", [P, 2, 512], fp32)) for n in range(2)]
        bank |= {n: ctx.enter_context(nc.psum_tensor(f"bank{n}", [P, 512], fp32)) for n in (6, 7)}

        x_in = sem("x_in")
        xT_in = [sem(f"xT_in{n}") for n in range(NB)]
        a0_in = [sem(f"a0_in{n}") for n in range(2)]
        scales_in = sem("scales_in")
        raw_in = sem("raw_in")
        bias_in = sem("bias_in")
        q_stacked = [sem(f"q_stacked{n}") for n in range(3)]
        k_stacked = [sem(f"k_stacked{n}") for n in range(3)]
        max_rows = sem("max_rows")
        stored = sem("stored")
        minus_rows = sem("minus_rows")
        v_ones = sem("v_ones")
        consts = sem("consts")
        gains = sem("gains")
        wa0_hi = sem("wa0_hi")
        wa0_lo = sem("wa0_lo")
        w_hi = sem("w_hi")
        w_lo = sem("w_lo")
        dn_scaled = sem("dn_scaled")
        bias_split = sem("bias_split")
        abs_done = sem("abs_done")
        sum_mm = sem("sum_mm")
        thresholds = sem("thresholds")
        below = sem("below")
        tern_done = sem("tern_done")
        qk_mm, v_mm, s_mm, mx_mm, st_mm = (sem(n) for n in ("qk_mm", "v_mm", "s_mm", "mx_mm", "st_mm"))
        pv_mm, ut_mm, yt_mm, o_mm, xt_mm = (sem(n) for n in ("pv_mm", "ut_mm", "yt_mm", "o_mm", "xt_mm"))
        gu_mm, d_mm = sem("gu_mm"), sem("d_mm")
        qk_hi = sem("qk_hi")
        qk_lo = sem("qk_lo")
        v_done = sem("v_done")
        max_taken = sem("max_taken")
        max_hi = sem("max_hi")
        max_split = sem("max_split")
        maxT_done = sem("maxT_done")
        exp_done = sem("exp_done")
        probs_done = sem("probs_done")
        u_done = sem("u_done")
        inv_done = sem("inv_done")
        y_done = sem("y_done")
        yT_hi_done = sem("yT_hi_done")
        yT_done = sem("yT_done")
        res_done = sem("res_done")
        var_done = sem("var_done")
        rstd_done = sem("rstd_done")
        ln_done = sem("ln_done")
        xT_hi_done = sem("xT_hi_done")
        xT_done = sem("xT_done")
        tanh_done = sem("tanh_done")
        gated = sem("gated")
        hf_done = sem("hf_done")
        hh_done = sem("hh_done")
        hl_done = sem("hl_done")
        dve_own = sem("dve_own")
        pool_own = sem("pool_own")

        def last_reader(step, k):
            kind, l, b, i = step
            n = count[step]
            return {"QK": (qk_lo, 2 * n - 1 + k), "V": (v_done, n), "MX": (maxT_done, n), "PV": (u_done, n),
                    "UT": (y_done, 2 * n - 1 + k), "YT": (yT_done, n), "XT": (xT_done, NB + n),
                    "O": (res_done, ln_of("O", l, b) if kind == "O" else 0),
                    "D": (res_done, ln_of("D", l, b) if kind == "D" else 0),
                    "S": (max_taken, 2 * n - 1 + k), "ST": (exp_done, n), "GU": (hf_done, n),
                    "TERN": (thresholds, i // TERN + 1)}[kind]

        IN_TURN = {"QK": 2, "V": 1, "MX": 1, "PV": 1, "UT": 2, "YT": 1, "O": 1, "XT": 1, "TERN": 1}
        banks_of, before, held, turn, pair_turn = {}, {}, {}, 0, 0
        for step in order:
            kind = step[0]
            if kind == "S":
                mine = [0, 1]
            elif kind == "D":
                mine = [step[2] % 2]
            elif kind in ("ST", "GU"):
                mine = [2 + pair_turn % 2]
                pair_turn += 1
            elif kind in IN_TURN and (kind != "TERN" or step[3] % TERN == 1):
                mine = [6 + (turn + k) % 2 for k in range(IN_TURN[kind])]
                turn += len(mine)
            else:
                mine = []
            banks_of[step] = mine
            before[step] = [held.get(n) for n in mine]
            for k, n in enumerate(mine):
                held[n] = (step, k)

        def place(step, k=0):
            n = banks_of[step][k]
            return pairs[n - 2] if n in (2, 3) else bank[n]

        def first_keys(a):
            return a.rearrange("p (c t) -> p c t", t=P)[:, 0:3:2, :]

        def xcols(b):
            return slice(b * T, (b + 1) * T)

        raw_a = raw[:, :].rearrange("p (k n) -> p k n", k=KT)
        W0 = MT0 * P

        def part_of_gate_up(k):
            kt, part = k // 2, k % 2
            return slice(part * W0, (part + 1) * W0), slice((2 * kt + part) * W0, (2 * kt + part + 1) * W0)

        def ternary_piece(step_no):
            m, r = step_no // TERN, step_no % TERN - 2
            c = slice(512 * r, 512 * (r + 1))
            return m, c, (gu_hi, gu_lo, dn)[m][:, c]

        block = ctx.enter_context(nc.Block())

        @block.sync
        def _(sp):
            for n in range(2):
                c = slice(n * 512, (n + 1) * 512)
                sp.dma_start(raw_a[:, :, c], a0[:, :, c]).then_inc(a0_in[n], 16)
                for b in (2 * n, 2 * n + 1):
                    sp.dma_start(xT_raw[:, :, xcols(b)], x_tr[:, :, xcols(b)]).then_inc(xT_in[b], 16)
            sp.dma_start(x[:, :, :], x_nat).then_inc(x_in, 16)
            sp.dma_start(gs_c[:, :], gs).then_inc(scales_in, 16)
            sp.dma_start(us_c[:, :], us).then_inc(scales_in, 16)
            sp.dma_start(ds_b[:, :], ds_row.partition_broadcast(P)).then_inc(scales_in, 16)
            sp.dma_start(qk_bias[:, :], bqk).then_inc(bias_in, 16)
            sp.dma_start(b_row[:, :], brow).then_inc(bias_in, 16)

            for step, l, b, i in order:
                if step == "PREPA":
                    sp.wait_ge(wa0_lo, 2)
                    sp.dma_start(raw[:, 0:2 * W0], f0gu[:, 0, :]).then_inc(raw_in, 16)
                if step == "PREP0" and i == 1:
                    sp.wait_ge(w_lo, 2)
                    sp.dma_start(raw[:, 0:2 * W0], f0gu[:, 1, :]).then_inc(raw_in, 16)
                if step == "PREP0" and i == 3:
                    sp.wait_ge(w_lo, 4)
                    sp.dma_start(raw[:, 0:MT0 * D], f0dn).then_inc(raw_in, 16)
                if step == "PREP0" and i == PREP0 - 1:
                    sp.wait_ge(dn_scaled, 3)
                    sp.dma_start(raw[:, :], a1).then_inc(raw_in, 16)
                if step == "PREP1" and i == PREP1 - 1:
                    sp.wait_ge(w_lo, PREP0 + PREP1)
                    sp.dma_start(raw[:, :], f1[:, 0, :]).then_inc(raw_in, 16)
                if step == "TERN" and i in (TERN - 1, 2 * TERN - 1):
                    m = i // TERN
                    sp.wait_ge(tern_done, 4 * (m + 1))
                    sp.dma_start(raw[:, :], f1[:, m + 1, :]).then_inc(raw_in, 16)
                if step == "QK":
                    n = b % 3
                    if users(l, b):
                        sp.wait_ge(st_mm, nth("ST", *users(l, b)[-1], NS - 1))
                    if l == 1 and b < 3:
                        sp.wait_ge(d_mm, nth("D", 0, NB - 2 if b < 2 else NB - 1))
                    if l == 0 and b < 3:
                        sp.wait_ge(minus_rows, n + 1)
                    sp.wait_ge(qk_hi, 2 * nth("QK", l, b))
                    sp.wait_ge(qk_lo, 2 * nth("QK", l, b))
                    for j in range(2):
                        for at, src in ((0, q_hi), (16, q_lo), (32, q_hi)):
                            r = 64 * j + at
                            sp.dma_start(q_stack[n][r:r + HD, :, :].bitcast(fp32),
                                         src[:, j, :].bitcast(fp32)).then_inc(q_stacked[n], 16)
                        for at, src in ((0, k_hi), (16, k_hi), (32, k_lo)):
                            r = 64 * j + at
                            sp.dma_start(k_stack[n][r:r + HD, :, :].bitcast(fp32),
                                         src[:, j, :].bitcast(fp32)).then_inc(k_stacked[n], 16)
                if step == "MX":
                    sp.wait_ge(maxT_done, nth("MX", l, b))
                    for j in range(2):
                        r = 64 * j + 3 * HD
                        sp.dma_start(q_stack[b % 3][r:r + 2, :, :].bitcast(fp32),
                                     maxT[H * j:H * (j + 1), :].bitcast(fp32)).then_inc(max_rows, 16)
                if step == "LN" and l == 3:
                    sp.wait_ge(ln_done, nth("LN", l, b))
                    sp.dma_start(out[:, TT * b:TT * (b + 1), :], x[:, TT * b:TT * (b + 1), :]).then_inc(stored, 16)
            sp.wait_ge(stored, 16 * NB)

        @block.tensor
        def _(pe):
            def take(step, k=0):
                if before[step][k]:
                    pe.wait_ge(*last_reader(*before[step][k]))
                return place(step, k)

            def three(o, w_hi, w_lo, m_hi, m_lo, first, last):
                nc.tensor.matmul(o, w_hi, m_hi, start=first, stop=False)
                nc.tensor.matmul(o, w_hi, m_lo, start=False, stop=False)
                return nc.tensor.matmul(o, w_lo, m_hi, start=False, stop=last)

            def tokens_by_features(o, a_hi, a_lo, base, cols, bias):
                for tt in range(TT):
                    tok = slice(base + tt * P, base + (tt + 1) * P)
                    oo = o[:, tt * D:(tt + 1) * D]
                    for kt in range(KT):
                        last = three(oo, a_hi[:, kt, tok], a_lo[:, kt, tok], wa_hi[:, kt, cols], wa_lo[:, kt, cols],
                                     kt == 0, kt == KT - 1 and bias is None)
                    if bias is not None:
                        nc.tensor.matmul(oo, ones_row[0:1, :], b_hi[0:1, bias], start=False, stop=False)
                        last = nc.tensor.matmul(oo, ones_row[0:1, :], b_lo[0:1, bias], start=False, stop=True)
                return last

            for step, l, b, i in order:
                key = (step, l, b, i)
                if step == "QK":
                    if l == 0:
                        pe.wait_ge(wa0_lo, 1)
                        pe.wait_ge(xT_done, b + 1)
                    else:
                        pe.wait_ge(w_lo, PREP0 + PREP1)
                        pe.wait_ge(xT_done, NB + nth("XT", 1, b))
                    for part in range(2):
                        o = take(key, part)
                        for j in range(2):
                            c = slice(part * D + j * P, part * D + (j + 1) * P)
                            for kt in range(KT):
                                last = three(o[:, j * T:(j + 1) * T], wa_hi[:, kt, c], wa_lo[:, kt, c],
                                             xT_hi[:, kt, xcols(b)], xT_lo[:, kt, xcols(b)], kt == 0, kt == KT - 1)
                        last.then_inc(qk_mm, 1)
                if step == "V":
                    if l == 0:
                        pe.wait_ge(wa0_lo, 2)
                    else:
                        pe.wait_ge(bias_split, 2)
                    tokens_by_features(take(key), xT_hi, xT_lo, b * T, slice(2 * D, 3 * D),
                                       slice(0, D) if l else None).then_inc(v_mm, 1)
                if step == "S":
                    n = b % 3
                    if i == 0:
                        pe.wait_ge(q_stacked[n], 96 * (len(users(l, b)) + 1))
                        pe.wait_ge(k_stacked[n], 96 * (len(users(l, b)) + 1))
                    for j in range(2):
                        o = take(key, j)
                        r = slice(64 * j, 64 * j + 3 * HD)
                        nc.tensor.matmul(o[:, 0:T], q_stack[n][r, i, P:T], k_stack[n][r, i, :], start=True, stop=True)
                        nc.tensor.matmul(o[:, T:T + P], q_stack[n][r, i, 0:P], k_stack[n][r, i, 0:P],
                                         start=True, stop=True).then_inc(s_mm, 1)
                if step == "MX":
                    pe.wait_ge(max_split, nth("MX", l, b))
                    pe.wait_ge(consts, 5)
                    o = take(key)
                    for qt in range(2):
                        last = nc.tensor.transpose(o[:, qt * P:(qt + 1) * P], max_hl[:, qt, :], ident[:, :])
                    last.then_inc(mx_mm, 1)
                if step == "ST":
                    n = b % 3
                    if i == 0:
                        pe.wait_ge(max_rows, 32 * nth("MX", l, b))
                    o = take(key)
                    for j in range(2):
                        r = slice(64 * j, 64 * j + 3 * HD + 2)
                        nc.tensor.matmul(first_keys(o[:, j, 0:T + P]), k_stack[n][r, i, 0:P],
                                         q_stack[n][r, i, :].rearrange("p (c t) -> p c t", t=P), start=True, stop=True)
                        last = nc.tensor.matmul(o[:, j, P:T], k_stack[n][r, i, P:T], q_stack[n][r, i, P:T],
                                                start=True, stop=True)
                    last.then_inc(st_mm, 1)
                if step == "PV":
                    pe.wait_ge(probs_done, nth("ST", l, b, 2 * i + 1))
                    if i == 0:
                        pe.wait_ge(v_done, nth("V", l, b))
                        pe.wait_ge(v_ones, 3)
                    o = take(key)
                    for kt in range(TT):
                        for g in range(4):
                            s, j = 2 * i + g // 2, g % 2
                            pr = probs[(nth("ST", l, b, s) - 1) % 4]
                            oo, v = o[32 * g:32 * g + 32, kt * P:T], v_aug[b % 3][:, kt, 8 * j + s, :]
                            if kt == 0:
                                last = nc.tensor.matmul(oo.rearrange("p (c t) -> p c t", t=P), v, first_keys(pr[:, j, :]),
                                                        start=True, stop=False)
                            else:
                                last = nc.tensor.matmul(oo, v, pr[:, j, P:T], start=False, stop=True)
                    last.then_inc(pv_mm, 1)
                if step == "UT":
                    pe.wait_ge(u_done, nth("PV", l, b, NGI - 1))
                    for qt in range(TT):
                        o = take(key, qt)
                        for gi in range(NGI):
                            last = nc.tensor.transpose(o[:, gi * P:(gi + 1) * P], u_sb[:, gi, qt * P:(qt + 1) * P],
                                                       ident[:, :])
                        last.then_inc(ut_mm, 1)
                if step == "YT":
                    pe.wait_ge(y_done, 2 * nth("UT", l, b))
                    o = take(key)
                    for kt in range(KT):
                        for tt in range(TT):
                            last = nc.tensor.transpose(o[:, kt * T + tt * P:kt * T + (tt + 1) * P],
                                                       y[:, tt, kt * P:(kt + 1) * P], ident[:, :])
                    last.then_inc(yt_mm, 1)
                if step == "O":
                    pe.wait_ge(yT_done, nth("YT", l, b))
                    tokens_by_features(take(key), yT_hi, yT_lo, 0, slice(3 * D, 4 * D),
                                       slice(D, 2 * D) if l else None).then_inc(o_mm, 1)
                if step == "XT":
                    pe.wait_ge(ln_done, nth("LN", l, b))
                    o = take(key)
                    for kt in range(KT):
                        for tt in range(TT):
                            last = nc.tensor.transpose(o[:, kt * T + tt * P:kt * T + (tt + 1) * P],
                                                       x[:, TT * b + tt, kt * P:(kt + 1) * P], ident[:, :])
                    last.then_inc(xt_mm, 1)
                if step == "GU":
                    if i == 0:
                        pe.wait_ge(xT_done, NB + nth("XT", 2 * l, b))
                        if b == 0 and l == 0:
                            pe.wait_ge(w_lo, PREP0)
                            pe.wait_ge(w_hi, PREP0)
                        if b == 0 and l == 1:
                            pe.wait_ge(tern_done, 12)
                    o2 = take(key)
                    for part in range(2):
                        for a in range(2):
                            mt = 2 * i + a
                            o = o2[:, part, a * T:(a + 1) * T]
                            for kt in range(KT):
                                x_hi, x_lo = xT_hi[:, kt, xcols(b)], xT_lo[:, kt, xcols(b)]
                                if l == 0:
                                    c = ((kt * 2 + part) * MT0 + mt) * P
                                    last = three(o, gu_hi[:, c:c + P], gu_lo[:, c:c + P], x_hi, x_lo,
                                                 kt == 0, kt == KT - 1)
                                else:
                                    w = (gu_hi, gu_lo)[part]
                                    c = kt * EXPERT + mt * P
                                    nc.tensor.matmul(o, w[:, c:c + P], x_hi, start=(kt == 0), stop=False)
                                    last = nc.tensor.matmul(o, w[:, c:c + P], x_lo, start=False, stop=(kt == KT - 1))
                    last.then_inc(gu_mm, 1)
                if step == "D":
                    nmt = (MT0, MT1)[l]
                    pe.wait_ge(hl_done, nth("GU", l, b, nmt // 2 - 1))
                    o = take(key)
                    h_hi, h_lo = hidden[b % 2]
                    for tt in range(TT):
                        tok = slice(tt * P, (tt + 1) * P)
                        oo = o[:, tt * D:(tt + 1) * D]
                        for kt in range(nmt):
                            w = dn[:, kt * D:(kt + 1) * D]
                            if l == 0:
                                last = three(oo, h_hi[:, kt, tok], h_lo[:, kt, tok], w,
                                             dn[:, (MT0 + kt) * D:(MT0 + kt + 1) * D], kt == 0, kt == nmt - 1)
                            else:
                                nc.tensor.matmul(oo, h_hi[:, kt, tok], w, start=(kt == 0), stop=False)
                                last = nc.tensor.matmul(oo, h_lo[:, kt, tok], w, start=False, stop=(kt == nmt - 1))
                    last.then_inc(d_mm, 1)
                if step == "TERN" and i % TERN == 1:
                    m = i // TERN
                    pe.wait_ge(abs_done, 4 * (m + 1))
                    nc.tensor.matmul(take(key)[:, 0:4], ones[:, :], abs_sum[:, m, :],
                                     start=True, stop=True).then_inc(sum_mm, 1)

        @block.scalar
        def _(act):
            for step, l, b, i in order:
                key = (step, l, b, i)
                if step == "PREPA":
                    for n in range(2):
                        c = slice(n * 512, (n + 1) * 512)
                        act.wait_ge(a0_in[n], 16)
                        nc.scalar.activation(wa_hi[:, :, c], raw_a[:, :, c], ACT.Copy).then_inc(wa0_hi, 1)
                        for bb in (2 * n, 2 * n + 1):
                            act.wait_ge(xT_in[bb], 16)
                            nc.scalar.activation(xT_hi[:, :, xcols(bb)], xT_raw[:, :, xcols(bb)],
                                                 ACT.Copy).then_inc(xT_hi_done, 1)
                if step == "QK":
                    k_ = nth("QK", l, b)
                    if k_ > 1:
                        pl, pb = batches[batches.index((l, b)) - 1]
                        act.wait_ge(q_stacked[pb % 3], 96 * (len(users(pl, pb)) + 1))
                        act.wait_ge(k_stacked[pb % 3], 96 * (len(users(pl, pb)) + 1))
                    if l == 1 and b == 0:
                        act.wait_ge(bias_in, 32)
                    for part, dst in ((0, q_hi), (1, k_hi)):
                        act.wait_ge(qk_mm, 2 * k_ - 1 + part)
                        src = place(key, part)[:, :].rearrange("p (j t) -> p j t", j=2)
                        if l == 0:
                            last = nc.scalar.activation(dst[:, :, :], src, ACT.Copy)
                        else:
                            for j in range(2):
                                last = nc.scalar.activation(dst[:, j, :], src[:, j, :], ACT.Identity,
                                                            bias=qk_bias[:, 2 * part + j:2 * part + j + 1])
                        last.then_inc(qk_hi, 1)
                if step == "V":
                    act.wait_ge(v_mm, nth("V", l, b))
                    if users(l, b):
                        act.wait_ge(pv_mm, nth("PV", *users(l, b)[-1], NGI - 1))
                    nc.scalar.activation(v_aug[b % 3][:, :, :, 0:HD].rearrange("p t h d -> p (t h) d"),
                                         place(key)[:, :].rearrange("p (th d) -> p th d", d=HD),
                                         ACT.Copy).then_inc(v_done, 1)
                if step == "MX":
                    act.wait_ge(mx_mm, nth("MX", l, b))
                    if nth("MX", l, b) > 1:
                        act.wait_ge(max_rows, 32 * (nth("MX", l, b) - 1))
                    nc.scalar.activation(maxT[:, :], place(key)[0:2 * H, 0:T], ACT.Copy).then_inc(maxT_done, 1)
                if step == "ST":
                    n = nth("ST", l, b, i)
                    act.wait_ge(st_mm, n)
                    if n > 4:
                        _, pl, pb, ps = st_steps[n - 5]
                        act.wait_ge(pv_mm, nth("PV", pl, pb, ps // 2))
                    nc.scalar.activation(probs[(n - 1) % 4][:, :, :], place(key)[:, :, 0:T + P], ACT.Exp,
                                         scale=SC).then_inc(exp_done, 1)
                if step == "PV":
                    act.wait_ge(pv_mm, nth("PV", l, b, i))
                    if i == 0 and (l, b) != (0, 0):
                        act.wait_ge(ut_mm, 2 * nth("UT", *batches[batches.index((l, b)) - 1]))
                    nc.scalar.activation(u_sb[:, i, :], place(key)[:, 0:T], ACT.Copy).then_inc(u_done, 1)
                if step == "YT":
                    act.wait_ge(yt_mm, nth("YT", l, b))
                    nc.scalar.activation(yT_hi[:, :, :], place(key)[:, :].rearrange("p (k t) -> p k t", k=KT),
                                         ACT.Copy).then_inc(yT_hi_done, 1)
                if step == "XT":
                    act.wait_ge(xt_mm, nth("XT", l, b))
                    nc.scalar.activation(xT_hi[:, :, xcols(b)], place(key)[:, :].rearrange("p (k t) -> p k t", k=KT),
                                         ACT.Copy).then_inc(xT_hi_done, 1)
                if step == "GU":
                    n = nth("GU", l, b, i)
                    act.wait_ge(gu_mm, n)
                    if n > 2:
                        act.wait_ge(gated, n - 2)
                    g = place(key)[:, 0, :]
                    if l == 0:
                        if n == 1:
                            act.wait_ge(gains, 2)
                        for a in range(2):
                            mt = 2 * i + a
                            last = nc.scalar.activation(th[n % 2][:, a * T:(a + 1) * T], g[:, a * T:(a + 1) * T],
                                                        ACT.Tanh, scale=half_gs[:, mt:mt + 1])
                    else:
                        last = nc.scalar.activation(th[n % 2][:, :], g, ACT.Tanh, scale=half[:, 0:1])
                    last.then_inc(tanh_done, 1)
                    if i == 0 and b < 2:
                        act.wait_ge(st_mm, nth("ST", l, NB - 1, NS - 1))
                        if l == 1 and b == 1:
                            act.wait_ge(d_mm, nth("D", 0, NB - 1))
                    if i == 0 and b >= 2:
                        act.wait_ge(d_mm, nth("D", l, b - 2))
                    act.wait_ge(hf_done, n)
                    nc.scalar.activation(hidden[b % 2][0][:, 2 * i:2 * i + 2, :],
                                         hf[n % 2][:, :].rearrange("p (a t) -> p a t", a=2), ACT.Copy).then_inc(hh_done, 1)
                if step == "PREP0":
                    if i < 4:
                        src, dst = part_of_gate_up(i)
                        act.wait_ge(raw_in, 16 * (i // 2 + 1))
                        nc.scalar.activation(gu_hi[:, dst], raw[:, src], ACT.Copy).then_inc(w_hi, 1)
                    else:
                        k_ = i - 4
                        act.wait_ge(dn_scaled, k_ + 1)
                        nc.scalar.activation(dn[:, k_ * 512:(k_ + 1) * 512], piece[i % 2][:, :], ACT.Copy).then_inc(w_hi, 1)
                if step == "PREP1":
                    c = slice(i * D, (i + 1) * D)
                    act.wait_ge(raw_in, 16 * 4)
                    if i == 0:
                        act.wait_ge(o_mm, nth("O", 0, NB - 1))
                    nc.scalar.activation(wa_hi[:, :, c], raw_a[:, :, c], ACT.Copy).then_inc(w_hi, 1)
                if step == "TERN" and i % TERN == 0:
                    m = i // TERN
                    act.wait_ge(raw_in, 16 * (5 + m))
                    if m == 0:
                        act.wait_ge(gated, nth("GU", 0, NB - 1, MT0 // 2 - 1))
                    for k_ in range(4):
                        if m or k_ > 1:
                            act.wait_ge(abs_done, 4 * m + k_ - 1)
                        nc.scalar.activation(junk[k_ % 2][:, :], raw[:, k_ * 512:(k_ + 1) * 512], ACT.Abs,
                                             accum_out=abs_sum[:, m, k_:k_ + 1]).then_inc(abs_done, 1)

        @block.vector
        def _(dve):
            links = [0]

            def link(ins):
                links[0] += 1
                ins.then_inc(dve_own, 1)
                dve.wait_ge(dve_own, links[0])

            def residual(step, l, b, gain_ap=None):
                n = ln_of(step, l, b)
                k_ = n % 2
                xb = x[:, TT * b:TT * (b + 1), :]
                o = place((step, l, b, 0))[:, :].rearrange("p (t d) -> p t d", t=TT)
                if gain_ap is None:
                    ins = nc.vector.tensor_tensor(res[k_][:, :, :], o, xb, ALU.add)
                else:
                    ins = nc.vector.scalar_tensor_tensor(res[k_][:, :, :], o, gain_ap, xb, ALU.mult, ALU.add)
                ins.then_inc(res_done, 1)
                dve.wait_ge(res_done, n)
                for tt in range(TT):
                    last = nc.vector.bn_stats(stats[k_][:, tt, :], res[k_][:, tt, :])
                link(last)
                for tt in range(TT):
                    last = nc.vector.bn_aggr(mv[k_][:, tt, :], stats[k_][:, tt, :])
                link(last)
                nc.vector.tensor_scalar(mv[k_][:, :, 1], mv[k_][:, :, 1], EPS, None, ALU.add).then_inc(var_done, 1)

            for step, l, b, i in order:
                key = (step, l, b, i)
                if step == "PREPA":
                    for n in range(2):
                        c = slice(n * 512, (n + 1) * 512)
                        dve.wait_ge(wa0_hi, n + 1)
                        nc.vector.tensor_tensor(wa_lo[:, :, c], raw_a[:, :, c], wa_hi[:, :, c].bitcast(fp32),
                                                ALU.subtract).then_inc(wa0_lo, 1)
                        for bb in (2 * n, 2 * n + 1):
                            dve.wait_ge(xT_hi_done, bb + 1)
                            nc.vector.tensor_tensor(xT_lo[:, :, xcols(bb)], xT_raw[:, :, xcols(bb)],
                                                    xT_hi[:, :, xcols(bb)].bitcast(fp32), ALU.subtract).then_inc(xT_done, 1)
                    dve.wait_ge(scales_in, 48)
                    nc.vector.tensor_scalar(half_gs[:, :], gs_c[:, :], 0.5, None, ALU.mult).then_inc(gains, 1)
                    dve.wait_ge(gains, 1)
                    nc.vector.tensor_tensor(gain[:, :], half_gs[:, :], us_c[:, :], ALU.mult).then_inc(gains, 1)
                    dve.wait_ge(bias_in, 32)
                    link(nc.vector.tensor_copy(b_hi[:, :], b_row[:, :]))
                    dve.wait_ge(consts, 1)
                    nc.vector.tensor_copy(ones_row[:, :], ones[0:1, :]).then_inc(bias_split, 1)
                    nc.vector.tensor_tensor(b_lo[:, :], b_row[:, :], b_hi[:, :].bitcast(fp32),
                                            ALU.subtract).then_inc(bias_split, 1)
                if step == "QK":
                    k_ = nth("QK", l, b)
                    for part, hi, lo in ((0, q_hi, q_lo), (1, k_hi, k_lo)):
                        dve.wait_ge(qk_hi, 2 * k_ - 1 + part)
                        src = place(key, part)[:, :].rearrange("p (j t) -> p j t", j=2)
                        if l == 0:
                            last = nc.vector.tensor_tensor(lo[:, :, :], src, hi[:, :, :].bitcast(fp32), ALU.subtract)
                        else:
                            for j in range(2):
                                last = nc.vector.scalar_tensor_tensor(lo[:, j, :], src[:, j, :],
                                                                      qk_bias[:, 2 * part + j:2 * part + j + 1],
                                                                      hi[:, j, :].bitcast(fp32), ALU.add, ALU.subtract)
                        last.then_inc(qk_lo, 1)
                if step == "S":
                    if nth("S", l, b, i) == 1:
                        dve.wait_ge(consts, 5)
                    for j in range(2):
                        n = 2 * nth("S", l, b, i) - 1 + j
                        dve.wait_ge(s_mm, n)
                        if n > 2:
                            dve.wait_ge(max_taken, n - 2)
                        o, h = place(key, j), 8 * j + i
                        nc.vector.tensor_tensor_reduce(out=masked[:, j, 0:T], in0=o[:, 0:T], in1=mask[:, 0:T], scale=1.0,
                                                       scalar=NEG, op0=ALU.add, op1=ALU.max,
                                                       accum_out=row_max[:, 1, h:h + 1])
                        nc.vector.tensor_tensor_reduce(out=masked[:, j, T:T + P], in0=o[:, T:T + P], in1=mask[:, T:T + P],
                                                       scale=1.0, scalar=NEG, op0=ALU.add, op1=ALU.max,
                                                       accum_out=row_max[:, 0, h:h + 1]).then_inc(max_taken, 1)
                if step == "MX":
                    n = nth("MX", l, b)
                    dve.wait_ge(max_taken, 2 * nth("S", l, b, NS - 1))
                    rm = row_max[:, :, :].rearrange("p q (j s) -> p (q j) s", j=2)
                    parts = max_hl[:, :, 0:2 * H].rearrange("p q (j c s) -> p q j c s", j=2, c=2)
                    for qt in range(2):
                        ins = nc.vector.tensor_copy(parts[:, qt, :, 0, :].bitcast(f32r), rm[:, 2 * qt:2 * qt + 2, :])
                    ins.then_inc(max_hi, 1)
                    dve.wait_ge(max_hi, n)
                    for qt in range(2):
                        ins = nc.vector.tensor_tensor(parts[:, qt, :, 1, :], rm[:, 2 * qt:2 * qt + 2, :],
                                                      parts[:, qt, :, 0, :], ALU.subtract)
                    ins.then_inc(max_split, 1)
                if step == "UT":
                    for qt in range(TT):
                        k_ = 2 * nth("UT", l, b) - 1 + qt
                        dve.wait_ge(ut_mm, k_)
                        o = place(key, qt)[:, :].rearrange("p (s j c) -> p j s c", s=NS, j=2)
                        inv = den_inv[:, qt, :].rearrange("p (j s) -> p j s", j=2)
                        nc.vector.reciprocal(inv, o[:, :, :, HD]).then_inc(inv_done, 1)
                        dve.wait_ge(inv_done, k_)
                        nc.vector.tensor_tensor(y[:, qt, :].rearrange("p (j s d) -> p j s d", j=2, s=NS), o[:, :, :, 0:HD],
                                                inv.unsqueeze(3).broadcast_to([P, 2, NS, HD]), ALU.mult).then_inc(y_done, 1)
                if step == "YT":
                    dve.wait_ge(yT_hi_done, nth("YT", l, b))
                    nc.vector.tensor_tensor(yT_lo[:, :, :], place(key)[:, :].rearrange("p (k t) -> p k t", k=KT),
                                            yT_hi[:, :, :].bitcast(fp32), ALU.subtract).then_inc(yT_done, 1)
                if step == "O":
                    dve.wait_ge(o_mm, nth("O", l, b))
                    if l == 0 and b == 0:
                        dve.wait_ge(x_in, 16)
                    residual("O", l, b)
                if step == "D":
                    dve.wait_ge(d_mm, nth("D", l, b))
                    residual("D", l, b, out_gain[:, 0:1] if l else None)
                if step == "LN":
                    n = nth("LN", l, b)
                    dve.wait_ge(rstd_done, n)
                    for tt in range(TT):
                        ins = nc.vector.tensor_scalar(x[:, TT * b + tt, :], res[n % 2][:, tt, :], mv[n % 2][:, tt, 0:1],
                                                      rstd[n % 2][:, tt:tt + 1], ALU.subtract, ALU.mult)
                    ins.then_inc(ln_done, 1)
                if step == "XT":
                    dve.wait_ge(xT_hi_done, NB + nth("XT", l, b))
                    nc.vector.tensor_tensor(xT_lo[:, :, xcols(b)], place(key)[:, :].rearrange("p (k t) -> p k t", k=KT),
                                            xT_hi[:, :, xcols(b)].bitcast(fp32), ALU.subtract).then_inc(xT_done, 1)
                if step == "GU":
                    n = nth("GU", l, b, i)
                    dve.wait_ge(tanh_done, n)
                    if n > 2:
                        dve.wait_ge(hl_done, n - 2)
                    o = place(key)
                    nc.vector.scalar_tensor_tensor(hf[n % 2][:, :], th[n % 2][:, :], 1.0, o[:, 0, :],
                                                   ALU.add, ALU.mult).then_inc(gated, 1)
                    dve.wait_ge(gated, n)
                    nc.vector.tensor_tensor(hf[n % 2][:, :], hf[n % 2][:, :], o[:, 1, :], ALU.mult).then_inc(hf_done, 1)
                if step == "PREP0" and i >= 4:
                    k_ = i - 4
                    dve.wait_ge(raw_in, 16 * 3)
                    if k_ == 0:
                        dve.wait_ge(gains, 2)
                    if k_ == 2:
                        dve.wait_ge(w_lo, 5)
                    for a in range(2):
                        kt = 2 * k_ + a
                        ins = nc.vector.scalar_tensor_tensor(piece[i % 2][:, a * D:(a + 1) * D], raw[:, kt * D:(kt + 1) * D],
                                                             gain[:, kt:kt + 1], ds_b[:, :], ALU.mult, ALU.mult)
                    ins.then_inc(dn_scaled, 1)
                if step == "TERN" and i % TERN == 1:
                    m = i // TERN
                    c = slice(m, m + 1)
                    dve.wait_ge(sum_mm, m + 1)
                    link(nc.vector.tensor_reduce(total[:, c], place(key)[:, 0:4], mybir.AxisListType.X, ALU.add))
                    link(nc.vector.tensor_scalar(scale[:, c], total[:, c], 1.0 / (D * EXPERT), QEPS, ALU.mult, ALU.add))
                    nc.vector.tensor_scalar(half[:, c], scale[:, c], 0.5, None, ALU.mult)
                    ins = nc.vector.tensor_scalar(minus[:, c], scale[:, c], -0.5, None, ALU.mult)
                    if m == 2:
                        link(nc.vector.tensor_tensor(out_gain[:, :], half[:, 0:1], scale[:, 1:2], ALU.mult))
                        ins = nc.vector.tensor_tensor(out_gain[:, :], out_gain[:, :], scale[:, 2:3], ALU.mult)
                    ins.then_inc(thresholds, 1)
                if step == "TERN" and i % TERN >= 2:
                    m, c, dst = ternary_piece(i)
                    n = 4 * m + i % TERN - 1
                    dve.wait_ge(below, n)
                    nc.vector.scalar_tensor_tensor(dst, raw[:, c], half[:, m:m + 1], piece[n % 2][:, :],
                                                   ALU.is_gt, ALU.subtract).then_inc(tern_done, 1)

        @block.gpsimd
        def _(pool):
            for n in range(3):
                pool.memset(k_stack[n][:, :, :].bitcast(fp32), -1.0).then_inc(minus_rows, 1)
            pool.memset(ones[:, :], 1.0).then_inc(consts, 1)
            pool.memset(max_hl[:, :, :], 0.0).then_inc(consts, 1)
            pool.memset(minus_half[:, :], -0.5)
            pool.memset(ident[:, :], 0.0).then_inc(pool_own, 1)
            pool.memset(mask[:, :], 0.0).then_inc(pool_own, 1)
            pool.wait_ge(pool_own, 2)
            pool.affine_select(out=ident[:, :], in_=ident[:, :], compare_op=ALU.not_equal, fill=1.0, base=0,
                               pattern=[[-1, P]], channel_multiplier=1).then_inc(consts, 1)
            pool.affine_select(out=mask[:, 0:T], in_=mask[:, 0:T], compare_op=ALU.is_ge, fill=NEG, base=P,
                               pattern=[[-1, T]], channel_multiplier=1).then_inc(consts, 1)
            pool.affine_select(out=mask[:, T:T + P], in_=mask[:, T:T + P], compare_op=ALU.is_ge, fill=NEG, base=0,
                               pattern=[[-1, P]], channel_multiplier=1).then_inc(consts, 1)
            for n in range(3):
                pool.memset(v_aug[n][:, :, :, HD:2 * HD], 1.0).then_inc(v_ones, 1)

            for step, l, b, i in order:
                if step == "ST":
                    n = nth("ST", l, b, i)
                    pool.wait_ge(exp_done, n)
                    diag = probs[(n - 1) % 4][:, :, 0:T]
                    pool.affine_select(out=diag, in_=diag, compare_op=ALU.is_ge, fill=0.0, base=0,
                                       pattern=[[0, 2], [0, 2], [1, P]], channel_multiplier=-1).then_inc(probs_done, 1)
                if step == "LN":
                    n = nth("LN", l, b)
                    pool.wait_ge(var_done, n)
                    pool.tensor_tensor(rstd[n % 2][:, :], mv[n % 2][:, :, 1], minus_half[:, :], ALU.pow).then_inc(rstd_done, 1)
                if step == "GU":
                    n = nth("GU", l, b, i)
                    pool.wait_ge(hh_done, n)
                    dst = hidden[b % 2]
                    pool.tensor_tensor(dst[1][:, 2 * i:2 * i + 2, :], hf[n % 2][:, :].rearrange("p (a t) -> p a t", a=2),
                                       dst[0][:, 2 * i:2 * i + 2, :].bitcast(fp32), ALU.subtract).then_inc(hl_done, 1)
                if step == "PREP0":
                    pool.wait_ge(w_hi, i + 1)
                    if i < 4:
                        src, dst = part_of_gate_up(i)
                        last = pool.tensor_tensor(gu_lo[:, dst], raw[:, src], gu_hi[:, dst].bitcast(fp32), ALU.subtract)
                    else:
                        k_ = i - 4
                        last = pool.tensor_tensor(dn[:, MT0 * D + k_ * 512:MT0 * D + (k_ + 1) * 512], piece[i % 2][:, :],
                                                  dn[:, k_ * 512:(k_ + 1) * 512].bitcast(fp32), ALU.subtract)
                    last.then_inc(w_lo, 1)
                if step == "PREP1":
                    c = slice(i * D, (i + 1) * D)
                    pool.wait_ge(w_hi, PREP0 + i + 1)
                    pool.tensor_tensor(wa_lo[:, :, c], raw_a[:, :, c], wa_hi[:, :, c].bitcast(fp32),
                                       ALU.subtract).then_inc(w_lo, 1)
                if step == "TERN" and i % TERN >= 2:
                    m, c, _ = ternary_piece(i)
                    n = 4 * m + i % TERN - 1
                    pool.wait_ge(thresholds, m + 1)
                    if n > 2:
                        pool.wait_ge(tern_done, n - 2)
                    pool.tensor_scalar(piece[n % 2][:, :], raw[:, c], minus[:, m:m + 1], None, ALU.is_lt).then_inc(below, 1)


_OUT = (NB, T, D)


def kernel(**inputs):
    import numpy as np
    import concourse.bacc as bacc
    from concourse.bass_utils import run_bass_kernel_spmd

    a = {k: np.asarray(v) for k, v in inputs.items()}

    def k_major(w):
        n, k = w.shape
        return np.ascontiguousarray(w.T.reshape(k // P, P, n).transpose(1, 0, 2))

    def by_stack(w):
        return w.reshape((2, NS, HD) + w.shape[1:]).swapaxes(1, 2).reshape(w.shape)

    def attention_weights(q, k, v, o):
        return np.concatenate([k_major(by_stack(q)), k_major(by_stack(k)), k_major(v), k_major(o)], axis=2)

    def by_partition(w, tiles):
        padded = np.zeros((tiles * P,) + w.shape[1:], w.dtype)
        padded[:w.shape[0]] = w
        return np.ascontiguousarray(padded.reshape((tiles, P) + w.shape[1:]).swapaxes(0, 1))

    wp = a["L0_attn_w_project"]
    gate_up = np.zeros((P, KT, 2, MT0 * P), np.float32)
    gate_up[..., 0, :INTER] = k_major(a["L0_ffn_gate_w"])
    gate_up[..., 1, :INTER] = k_major(a["L0_ffn_up_w"])
    tokens = a["L0_attn_x"].reshape(NB * T, D)
    bias = np.stack([by_stack(a["L1_attn_bq"]).reshape(2, P), by_stack(a["L1_attn_bk"]).reshape(2, P)])
    arrays = {
        "x_nat": tokens.reshape(NB * TT, P, D).transpose(1, 0, 2),
        "x_tr": k_major(tokens),
        "a0": attention_weights(wp[:D], wp[D:2 * D], wp[2 * D:], a["L0_attn_w_out"]),
        "f0gu": gate_up.reshape(P, KT, 2 * MT0 * P),
        "f0dn": by_partition(a["L0_ffn_down_w"].T, MT0).reshape(P, MT0 * D),
        "gs": by_partition(a["L0_ffn_gate_s"], MT0),
        "us": by_partition(a["L0_ffn_up_s"], MT0),
        "ds": a["L0_ffn_down_s"],
        "a1": attention_weights(a["L1_attn_Wq"], a["L1_attn_Wk"], a["L1_attn_Wv"], a["L1_attn_Wo"]).reshape(P, 4 * KT * D),
        "bqk": bias.reshape(4, P).T,
        "brow": np.concatenate([a["L1_attn_bv"], a["L1_attn_bo"]]).reshape(1, 2 * D),
        "f1": np.stack([k_major(a["L1_ffn_W_up"]).reshape(P, -1), k_major(a["L1_ffn_W_gate"]).reshape(P, -1),
                        k_major(a["L1_ffn_W_down"]).reshape(P, -1)], axis=1),
    }
    arrays = {k: np.ascontiguousarray(v) for k, v in arrays.items()}
    nc = bacc.Bacc("TRN2", target_bir_lowering=False, num_devices=1)
    aps = [nc.dram_tensor(k, v.shape, fp32, kind="ExternalInput").ap() for k, v in arrays.items()]
    out = nc.dram_tensor("out", (P, NB * TT, D), fp32, kind="ExternalOutput").ap()
    program(nc, *aps, out)
    r = run_bass_kernel_spmd(nc, [arrays], core_ids=[0])
    y = r.results[0]["out"]
    return np.ascontiguousarray(y.transpose(1, 0, 2)).reshape(_OUT)
```

```python
from contextlib import ExitStack

import concourse.bass as bass
from concourse import mybir

fp32 = mybir.dt.float32
f32r = mybir.dt.float32r
bf16 = mybir.dt.bfloat16
ALU = mybir.AluOpType
ACT = mybir.ActivationFunctionType

NB, T, D = 4, 256, 256
H, HD = 16, 16
NS = 8
P = 128
KT = D // P
TT = T // P
INTER = 704
MT0 = -(-INTER // P)
EXPERT = 1024
MT1 = EXPERT // P
EPS = 1e-5
QEPS = 1e-8
SC = 1.0 / HD ** 0.5
NEG = -3.0e38
NGI = 4

Q_BLOCKS = (0, 0, 1, 0, 1, 2)
K_BLOCKS = (0, 1, 0, 2, 1, 0)
KP = len(Q_BLOCKS) * HD

PREP0 = 7
PREP1 = 4
TERN = 6


TENSOR_STEPS = """
    QK:000-1 V:000 V:010 QK:010 V:020 QK:011 S:000-5 QK:020 S:006 QK:021 S:007 S:010 MX:000 S:011-3 ST:000 QK:030
    S:014 ST:001 QK:031 PV:000 S:015 ST:002-3 S:016 ST:004 S:017 ST:005 S:020 ST:006 S:021 PV:001-2 MX:010 S:022-3
    ST:007 S:024-5 ST:010 PV:003 S:026 ST:011 UT:000 V:030 ST:012 S:027 ST:013 YT:000 MX:020 ST:014-5 S:030-1 PV:010
    S:032-3 PV:011 S:034-5 ST:016-7 PV:012 S:036-7 ST:020 O:000 ST:021 PV:013 ST:022-3 UT:010 MX:030 ST:024 PV:020
    YT:010 PV:021 XT:000 ST:025-6 O:010 ST:027 PV:022 ST:030 GU:000 PV:023 ST:031-2 XT:010 ST:033 UT:020 ST:034
    PV:030 ST:035 YT:020 GU:001 PV:031 ST:036 PV:032 ST:037 GU:002 O:020 PV:033 GU:010 UT:030 D:000 YT:030 XT:020
    GU:011 O:030 GU:012 XT:100 GU:020-2 QK:100-1 XT:030 D:010 D:020 XT:110 GU:030 S:100-1 GU:031 S:102-4 GU:032
    S:105-7 QK:110-1 V:100 MX:100 XT:120 D:030 TERN:101 V:110 QK:120 ST:100 XT:130 ST:101 QK:121 S:110 ST:102 V:120
    S:111 ST:103-4 S:112-3 PV:100 S:114 ST:105 PV:101 QK:130 S:115 QK:131 S:116 PV:102 ST:106-7 S:117 S:120-1 PV:103
    V:130 TERN:107 MX:110 UT:100 S:122 YT:100 ST:110 S:123 ST:111-2 S:124 ST:113 S:125-7 ST:114-5 PV:110-1 ST:116
    MX:120 S:130 O:100 ST:117 S:131 ST:120 PV:112 ST:121 PV:113 S:132 ST:122-3 S:133 XT:200 ST:124 S:134 UT:110
    PV:120 S:135 ST:125 PV:121 S:136 ST:126 S:137 ST:127 TERN:1013 PV:122 YT:110 PV:123 MX:130 O:110 UT:120 ST:130-2
    YT:120 ST:133 PV:130 XT:210 ST:134-5 O:120 PV:131-2 ST:136-7 GU:100 XT:220 PV:133 GU:101 UT:130 GU:102-3 YT:130
    GU:110-2 D:100 GU:113 GU:120 O:130 GU:121 D:110 XT:230 GU:122-3 GU:130-3 D:120 D:130
"""
SCALAR_STEPS = """
    PREPA:000 XPARTS:000 PREPA:001 QK:000 PREPA:002 XPARTS:010 SPLIT:000 PREPA:003 QK:001 SPLIT:001 XPARTS:020 V:000
    PREP0:000 XPARTS:030 V:010 V:020 QK:010 SPLIT:010 QK:011 PREP0:001 SPLIT:011 QK:020 PREP0:002-3 SPLIT:020 QK:021
    MX:000 SPLIT:021 QK:030 ST:000-1 PREP0:004 SPLIT:030 QK:031 PREP0:005 PV:000 ST:002 SPLIT:031 ST:003-5 PV:001
    ST:006 PV:002 MX:010 PREP0:006 ST:007 ST:010 PV:003 ST:011 V:030 ST:012-3 YT:000 MX:020 PV:010 ST:014-5 PV:011
    ST:016 PV:012 ST:017 ST:020-1 PV:013 ST:022 MX:030 ST:023-4 PV:020 YT:010 PV:021 XT:000 ST:025-7 PV:022 ST:030
    GU:000 PV:023 ST:031 XT:010 ST:032 HI:000 ST:033 PV:030 ST:034 YT:020 ST:035 GU:001 PV:031 ST:036 HI:001 PV:032
    ST:037 GU:002 PV:033 HI:002 GU:010 HI:010 YT:030 XT:020 GU:011 PREP1:000-1 GU:012 PREP1:002 XT:100 PREP1:003
    HI:011-2 GU:020-1 HI:020-1 GU:022 QK:100 XT:030 HI:022 QK:101 SPLIT:100-1 XT:110 GU:030-1 HI:030 GU:032 HI:031
    QK:110 HI:032 QK:111 SPLIT:110 TERN:100 XT:120 V:100 SPLIT:111 MX:100 V:110 QK:120 ST:100 XT:130 SPLIT:120
    QK:121 ST:101-2 V:120 SPLIT:121 ST:103 PV:100 ST:104 PV:101 ST:105 QK:130-1 SPLIT:130 PV:102 ST:106-7 SPLIT:131
    TERN:106 PV:103 V:130 MX:110 YT:100 ST:110-4 PV:110-1 MX:120 ST:115-7 ST:120 PV:112 ST:121 PV:113 ST:122 XT:200
    ST:123 TERN:1012 PV:120 ST:124-5 PV:121 ST:126-7 YT:110 PV:122-3 MX:130 ST:130-2 YT:120 ST:133 XT:210 ST:134-5
    PV:130-2 ST:136-7 GU:100 XT:220 PV:133 GU:101 HI:100-1 GU:102-3 HI:102 GU:110 YT:130 HI:103 GU:111 HI:110 GU:112
    HI:111-2 GU:113 GU:120 HI:113 GU:121 HI:120-1 XT:230 GU:122-3 HI:122 GU:130 HI:123 GU:131 HI:130 GU:132 HI:131
    GU:133 HI:132-3
"""
VECTOR_STEPS = """
    PREPA:000 XPARTS:000 PREPA:001 QK:000 XPARTS:010 PREPA:002-3 QK:001 XPARTS:020 XPARTS:030 SCALES:000 QK:010
    S:000 QK:011 S:001-5 QK:020 S:006-7 QK:021 MX:000 S:010-3 PREP0:004 S:014 QK:030 PREP0:005 QK:031 S:015-7 MX:010
    S:020-1 PREP0:006 S:022-6 UT:000 S:027 MX:020 YT:000 S:030-7 MX:030 O:000 UT:010 LN:000 YT:010 XT:000 O:010
    LN:010 GU:000 XT:010 UT:020 YT:020 GU:001-2 O:020 UT:030 LN:020 GU:010 D:000 YT:030 GU:011 LN:100 XT:020 O:030
    GU:012 XT:100 LN:030 GU:020-2 QK:100-1 D:010 LN:110 XT:030 D:020 XT:110 LN:120 S:100-1 GU:030 S:102-3 GU:031
    S:104-6 GU:032 S:107 QK:110 MX:100 QK:111 XT:120 D:030 TERN:101 LN:130 QK:120 TERN:102 XT:130 S:110 QK:121
    TERN:103 S:111-4 TERN:104-5 S:115 QK:130-1 S:116-7 S:120-1 MX:110 TERN:107 UT:100 S:122 YT:100 TERN:108 S:123-7
    MX:120 TERN:109-10 S:130 TERN:1011 O:100 S:131 LN:200 S:132-3 XT:200 S:134 UT:110 S:135-7 TERN:1013 MX:130
    YT:110 TERN:1014 O:110 UT:120 LN:210 TERN:1015-16 YT:120 XT:210 TERN:1017 O:120 LN:220 GU:100-1 XT:220 UT:130
    GU:102-3 YT:130 GU:110-2 D:100 GU:113 LN:300 O:130 GU:120 LN:230 GU:121 D:110 XT:230 GU:122-3 GU:130-3 LN:310
    D:120 LN:320 D:130 LN:330
"""
GPSIMD_STEPS = """
    SPLIT:000-1 PREP0:000 SPLIT:010 PREP0:001 SPLIT:011 PREP0:002-3 SPLIT:020-1 ST:000-1 PREP0:004 ST:002-3
    PREP0:005 ST:004-5 SPLIT:030 ST:006 PREP0:006 ST:007 ST:010-1 SPLIT:031 ST:012-7 ST:020-1 LN:000 ST:022-7 LN:010
    ST:030-1 HI:000 ST:032-7 HI:001-2 LN:020 LN:100 HI:010 PREP1:000-1 LN:030 HI:011-2 PREP1:002-3 HI:020-2
    SPLIT:100-1 LN:110 LN:120 HI:030-2 SPLIT:110-1 LN:130 TERN:102-3 SPLIT:120 ST:100-2 SPLIT:121 ST:103 TERN:104-5
    ST:104-5 SPLIT:130 ST:106-7 TERN:108-10 SPLIT:131 ST:110-4 TERN:1011 ST:115-7 LN:200 ST:120-7 TERN:1014-16
    LN:210 ST:130-2 TERN:1017 ST:133-5 LN:220 ST:136-7 HI:100-3 HI:110-2 LN:300 HI:113 LN:230 HI:120-3 HI:130-1
    LN:310 HI:132-3 LN:320 LN:330
"""
SYNC_STEPS = """
    MINUS:000-2 QK:000 PREPA:003 QK:001 SPLIT:000-1 SCALES:000 QK:010 SPLIT:010 PREP0:001 SPLIT:011 QK:011 QK:020
    MX:000 PREP0:003 SPLIT:020 QK:021 SPLIT:021 QK:030 MX:010 QK:031 SPLIT:030-1 MX:020 MX:030 PREP0:006 QK:100
    SPLIT:100-1 QK:101 PREP1:003 QK:110 SPLIT:110-1 MX:100 QK:111 SPLIT:120 QK:120 SPLIT:121 QK:121 TERN:105
    QK:130-1 SPLIT:130 MX:110 SPLIT:131 MX:120 TERN:1011 MX:130 LN:300 LN:310 LN:320 LN:330
"""


def steps(text):
    found = []
    for word in text.split():
        kind, at = word.split(":")
        first, _, last = at[2:].partition("-")
        found += [(kind, int(at[0]), int(at[1]), part) for part in range(int(first), int(last or first) + 1)]
    return found


def program(nc, x_nat, x_tr, a0, f0gu, f0dn, gs, us, ds_row, a1, bqk, brow, f1, out):
    order, act_order, dve_order, pool_order, sp_order = (
        steps(text) for text in (TENSOR_STEPS, SCALAR_STEPS, VECTOR_STEPS, GPSIMD_STEPS, SYNC_STEPS))
    walked = (order, dve_order, act_order, pool_order, sp_order)
    count = {}
    for kind in {q[0] for w in walked for q in w}:
        runs = [[q for q in w if q[0] == kind] for w in walked]
        run = max(runs, key=len) if kind in ("LN", "XT") else sorted({q for r in runs for q in r})
        assert all(r == [q for q in run if q in r] for r in runs), kind
        count.update({q: n + 1 for n, q in enumerate(run)})

    def nth(step, l=0, b=0, i=0):
        return count[(step, l, b, i)]

    st_steps = [q for q in order if q[0] == "ST"]
    of_residual = [q for q in dve_order if q[0] in ("O", "D", "LN")]
    assert all(q[1:3] == (2 * p[1] + (p[0] == "D"), p[2]) for p, q in zip(of_residual[::2], of_residual[1::2]))

    def ln_of(step, l, b):
        return nth("LN", 2 * l + (step == "D"), b)

    batches = [(l, b) for l in range(2) for b in range(NB)]

    def users(l, b):
        return [q for q in batches if q < (l, b) and q[1] % 3 == b % 3]

    ctx = ExitStack()
    with ctx:
        def sb(name, shape, dt=fp32):
            return ctx.enter_context(nc.sbuf_tensor(name, shape, dt))

        def sem(name):
            return ctx.enter_context(nc.semaphore(name))

        x = sb("x", [P, NB * TT, D])
        xT_hi = sb("xT_hi", [P, KT, NB * T], f32r)
        xT_lo = sb("xT_lo", [P, KT, NB * T], f32r)
        ident = sb("ident", [P, P])
        ident_b = sb("ident_b", [P, P], bf16)
        mask = sb("mask", [P, 384])
        ones = sb("ones", [P, P])
        minus_ones = sb("minus_ones", [P, 2 * H * T // P], bf16)
        ones_rows = sb("ones_rows", [2, P], f32r)
        raw = sb("raw", [P, 2048])
        wa_hi = sb("wa_hi", [P, KT, 4 * D], f32r)
        wa_lo = sb("wa_lo", [P, KT, 4 * D], f32r)
        gu_hi = sb("gu_hi", [P, KT * 2 * MT0 * P], f32r)
        gu_lo = sb("gu_lo", [P, KT * 2 * MT0 * P], f32r)
        dn = sb("dn", [P, 2 * MT0 * D], f32r)
        qk_bias = sb("qk_bias", [P, 4])
        b_parts = sb("b_parts", [2, 2 * D], f32r)
        b_lo = sb("b_lo", [1, 2 * D], f32r)
        gs_c = sb("gs_c", [P, MT0])
        us_c = sb("us_c", [P, MT0])
        half_gs = sb("half_gs", [P, MT0])
        gain = sb("gain", [P, MT0])
        ds_b = sb("ds_b", [P, D])
        part_of = [[sb(f"{name}_part{n}", [P, 2 * T], bf16) for n in range(3)] for name in "qk"]
        left = [sb(f"{name}_left", [P, 2 * T]) for name in "qk"]
        q_region = sb("q_region", [P, NB * NS, T], f32r)
        q_stacks = q_region[:, :, :].rearrange("p n t -> p (n t)").bitcast(bf16).rearrange("p (n h t) -> p n h t", n=NB, h=H)
        q_stack = [q_stacks[:, n, :, :] for n in range(NB)]
        k_stack = [sb(f"k_stack{n}", [P, H, T], bf16) for n in range(3)]
        v_aug = [sb(f"v_aug{n}", [P, TT, H, 2 * HD]) for n in range(3)]
        masked = sb("masked", [P, 2, T + P], bf16)
        row_max = [sb(f"row_max{n}", [P, 2, H]) for n in range(2)]
        max_hl = sb("max_hl", [P, 2, 2, H], bf16)
        maxT = sb("maxT", [2 * H, T], bf16)
        probs_all = sb("probs", [P, 4 * 2 * (T + P)])
        probs = [probs_all[:, n * 2 * (T + P):(n + 1) * 2 * (T + P)].rearrange("p (j t) -> p j t", j=2) for n in range(4)]
        xT_raw = probs_all[:, 0:KT * NB * T].rearrange("p (k t) -> p k t", k=KT)
        u_sb = sb("u_sb", [P, NGI, T])
        den_inv = sb("den_inv", [P, 2, H])
        y = sb("y", [P, TT, D])
        yT_hi = sb("yT_hi", [P, KT, T], f32r)
        yT_lo = sb("yT_lo", [P, KT, T], f32r)
        res = [sb(f"res{n}", [P, TT, D]) for n in range(2)]
        stats = [sb(f"stats{n}", [P, TT, 6]) for n in range(2)]
        mv = [sb(f"mv{n}", [P, TT, 2]) for n in range(2)]
        rstd = [sb(f"rstd{n}", [P, TT]) for n in range(2)]
        minus_half = sb("minus_half", [P, TT])
        th = [sb(f"th{n}", [P, 512]) for n in range(2)]
        hf = [sb(f"hf{n}", [P, 512]) for n in range(2)]
        piece, junk, b_row = hf, th, th[1][0:1, :]

        def hidden(l, b, part, kt):
            if l == 0:
                at = MT0 * (2 * (b % 2) + part) + kt
                return q_region[:, at:at + 2, :]
            if b % 2 == 0 or part == 0:
                at = NS * (1 if b % 2 else (3, 0)[part]) + kt
                return q_region[:, at:at + 2, :]
            at = KT * EXPERT + kt % 4 * T
            return (gu_hi, gu_lo)[kt // 4][:, at:at + 2 * T].rearrange("p (a t) -> p a t", a=2)

        abs_sum = sb("abs_sum", [P, 3, 4])
        scale = sb("scale", [P, 3])
        half = sb("half", [P, 3])
        minus = sb("minus", [P, 3])
        total = sb("total", [P, 3])
        out_gain = sb("out_gain", [P, 1])

        pairs = [ctx.enter_context(nc.psum_tensor(f"pair{n}", [P, 2, 512], fp32)) for n in range(4)]

        x_in = sem("x_in")
        xT_in = [sem(f"xT_in{n}") for n in range(NB)]
        a0_in = [sem(f"a0_in{n}") for n in range(4)]
        scales_in = sem("scales_in")
        raw_in = sem("raw_in")
        bias_in = sem("bias_in")
        q_stacked = [sem(f"q_stacked{n}") for n in range(NB)]
        k_stacked = [sem(f"k_stacked{n}") for n in range(3)]
        max_rows = sem("max_rows")
        stored = sem("stored")
        minus_rows = sem("minus_rows")
        v_ones = sem("v_ones")
        consts = sem("consts")
        gains = sem("gains")
        wa0_hi = sem("wa0_hi")
        wa0_lo = sem("wa0_lo")
        w_hi = sem("w_hi")
        w_lo = sem("w_lo")
        dn_scaled = sem("dn_scaled")
        bias_split = sem("bias_split")
        bias_moved = sem("bias_moved")
        abs_done = sem("abs_done")
        sum_mm = sem("sum_mm")
        thresholds = sem("thresholds")
        below = sem("below")
        tern_done = sem("tern_done")
        qk_mm, v_mm, s_mm, mx_mm, st_mm = (sem(n) for n in ("qk_mm", "v_mm", "s_mm", "mx_mm", "st_mm"))
        pv_mm, ut_mm, yt_mm, o_mm, xt_mm = (sem(n) for n in ("pv_mm", "ut_mm", "yt_mm", "o_mm", "xt_mm"))
        gu_mm, d_mm = sem("gu_mm"), sem("d_mm")
        qk_hi = sem("qk_hi")
        qk_left = sem("qk_left")
        qk_mid = sem("qk_mid")
        qk_lo = sem("qk_lo")
        v_done = sem("v_done")
        max_taken = sem("max_taken")
        max_hi = sem("max_hi")
        max_split = sem("max_split")
        maxT_done = sem("maxT_done")
        exp_done = sem("exp_done")
        probs_done = sem("probs_done")
        u_done = sem("u_done")
        inv_done = sem("inv_done")
        y_done = sem("y_done")
        yT_hi_done = sem("yT_hi_done")
        yT_done = sem("yT_done")
        res_done = sem("res_done")
        var_done = sem("var_done")
        rstd_done = sem("rstd_done")
        ln_done = sem("ln_done")
        xT_hi_done = sem("xT_hi_done")
        xT_done = sem("xT_done")
        tanh_done = sem("tanh_done")
        gated = sem("gated")
        hf_done = sem("hf_done")
        hh_done = sem("hh_done")
        hl_done = sem("hl_done")
        dve_own = sem("dve_own")
        pool_own = sem("pool_own")

        def last_reader(step, k):
            kind, l, b, i = step
            n = count[step]
            return {"QK": (qk_left, n), "V": (v_done, n), "MX": (maxT_done, n), "PV": (u_done, n),
                    "UT": (y_done, 2 * n - 1 + k), "YT": (yT_done, n), "XT": (xT_done, NB + n),
                    "O": (res_done, ln_of("O", l, b) if kind == "O" else 0),
                    "D": (res_done, ln_of("D", l, b) if kind == "D" else 0),
                    "S": (max_taken, 2 * n - 1 + k), "ST": (exp_done, n), "GU": (hf_done, n),
                    "TERN": (thresholds, i // TERN + 1)}[kind]

        SINGLE = {"S": 2, "D": 1, "QK": 1, "V": 1, "MX": 1, "PV": 1, "UT": 2, "YT": 1, "O": 1, "XT": 1, "TERN": 1}
        banks_of, before, held, taken = {}, {}, {}, {n: -8 + n for n in range(8)}
        for now, step in enumerate(order):
            kind, choices, mine = step[0], [], []
            if kind in ("ST", "GU"):
                choices = [(2, 3), (4, 5)] + ([(0, 1)] if kind == "GU" else [])
            elif kind in SINGLE and (kind != "TERN" or step[3] % TERN == 1):
                choices = [(n,) for n in (0, 1, 6, 7)]
            for k in range(SINGLE.get(kind, 1) if choices else 0):
                mine.append(min(choices, key=lambda c: max(taken[n] for n in c)))
                taken.update({n: now + 0.5 * k for n in mine[-1]})
            banks_of[step] = mine
            before[step] = [{held[n] for n in c if n in held} for c in mine]
            held.update({n: (step, k) for k, c in enumerate(mine) for n in c})

        def place(step, k=0):
            c = banks_of[step][k]
            return pairs[c[0] // 2] if len(c) == 2 else pairs[c[0] // 2][:, c[0] % 2, :]

        def first_keys(a):
            return a.rearrange("p (c t) -> p c t", t=P)[:, 0:3:2, :]

        def xcols(b):
            return slice(b * T, (b + 1) * T)

        raw_a = raw[:, :].rearrange("p (k n) -> p k n", k=KT)
        W0 = MT0 * P

        def part_of_gate_up(k):
            kt, part = k // 2, k % 2
            return slice(part * W0, (part + 1) * W0), slice((2 * kt + part) * W0, (2 * kt + part + 1) * W0)

        def ternary_piece(step_no):
            m, r = step_no // TERN, step_no % TERN - 2
            c = slice(512 * r, 512 * (r + 1))
            return m, c, (gu_hi, gu_lo, dn)[m][:, c]

        block = ctx.enter_context(nc.Block())

        @block.sync
        def _(sp):
            for n, b in enumerate((0, None, 1, None)):
                c = slice(n * D, (n + 1) * D)
                sp.dma_start(raw_a[:, :, c], a0[:, :, c]).then_inc(a0_in[n], 16)
                if b is not None:
                    sp.dma_start(xT_raw[:, :, xcols(b)], x_tr[:, :, xcols(b)]).then_inc(xT_in[b], 16)
            for b in range(2, NB):
                sp.dma_start(xT_raw[:, :, xcols(b)], x_tr[:, :, xcols(b)]).then_inc(xT_in[b], 16)
            sp.dma_start(x[:, :, :], x_nat).then_inc(x_in, 16)
            sp.dma_start(gs_c[:, :], gs).then_inc(scales_in, 16)
            sp.dma_start(us_c[:, :], us).then_inc(scales_in, 16)
            sp.dma_start(ds_b[:, :], ds_row.partition_broadcast(P)).then_inc(scales_in, 16)
            sp.dma_start(qk_bias[:, :], bqk).then_inc(bias_in, 16)
            sp.dma_start(b_row[:, :], brow).then_inc(bias_in, 16)

            for step, l, b, i in sp_order:
                if step == "PREPA" and i == 3:
                    sp.wait_ge(wa0_lo, 4)
                    sp.dma_start(raw[:, 0:2 * W0], f0gu[:, 0, :]).then_inc(raw_in, 16)
                if step == "PREP0" and i == 1:
                    sp.wait_ge(w_lo, 2)
                    sp.dma_start(raw[:, 0:2 * W0], f0gu[:, 1, :]).then_inc(raw_in, 16)
                if step == "PREP0" and i == 3:
                    sp.wait_ge(w_lo, 4)
                    sp.dma_start(raw[:, 0:MT0 * D], f0dn).then_inc(raw_in, 16)
                if step == "PREP0" and i == PREP0 - 1:
                    sp.wait_ge(dn_scaled, 3)
                    sp.dma_start(raw[:, :], a1).then_inc(raw_in, 16)
                if step == "PREP1" and i == PREP1 - 1:
                    sp.wait_ge(w_lo, PREP0 + PREP1)
                    sp.dma_start(raw[:, :], f1[:, 0, :]).then_inc(raw_in, 16)
                if step == "TERN" and i in (TERN - 1, 2 * TERN - 1):
                    m = i // TERN
                    sp.wait_ge(tern_done, 4 * (m + 1))
                    sp.dma_start(raw[:, :], f1[:, m + 1, :]).then_inc(raw_in, 16)
                if step == "MINUS":
                    sp.wait_ge(consts, 1)
                    sp.dma_start(k_stack[i][KP:KP + 2, :, :].rearrange("p h t -> p (h t)"),
                                 minus_ones[:, :]).then_inc(minus_rows, 16)
                if step in ("QK", "SPLIT"):
                    n = (b - l) % NB
                    stack, stacked, blocks = ((q_stack[n], q_stacked[n], Q_BLOCKS),
                                              (k_stack[b % 3], k_stacked[b % 3], K_BLOCKS))[i]
                if step == "QK":
                    if i == 0 and l == 1 and b == 0:
                        sp.wait_ge(st_mm, nth("ST", 0, NB - 1, NS - 1))
                    if i == 0 and l == 1 and b > 0:
                        sp.wait_ge(d_mm, nth("D", 0, NB - 2 if b == 1 else NB - 1))
                    if i == 1 and users(l, b):
                        sp.wait_ge(st_mm, nth("ST", *users(l, b)[-1], NS - 1))
                    sp.wait_ge(qk_hi, nth("QK", l, b, i))
                    for r in range(len(blocks)):
                        if blocks[r] == 0:
                            sp.dma_start(stack[HD * r:HD * (r + 1), :, :].rearrange("p h t -> p (h t)"),
                                         part_of[i][0][:, :]).then_inc(stacked, 16)
                if step == "SPLIT":
                    for n, done in ((1, qk_mid), (2, qk_lo)):
                        sp.wait_ge(done, nth("SPLIT", l, b, i))
                        for r in range(len(blocks)):
                            if blocks[r] == n:
                                sp.dma_start(stack[HD * r:HD * (r + 1), :, :].rearrange("p h t -> p (h t)"),
                                             part_of[i][n][:, :]).then_inc(stacked, 16)
                if step == "SCALES":
                    sp.wait_ge(bias_split, 2)
                    sp.dma_start(b_parts[1:2, :].bitcast(fp32), b_lo[:, :].bitcast(fp32)).then_inc(bias_moved, 16)
                if step == "MX":
                    sp.wait_ge(maxT_done, nth("MX", l, b))
                    sp.dma_start(q_stack[(b - l) % NB][KP:KP + 2, :, :].rearrange("p h t -> p (h t)"),
                                 maxT[:, :]).then_inc(max_rows, 16)
                if step == "LN" and l == 3:
                    sp.wait_ge(ln_done, nth("LN", l, b))
                    sp.dma_start(out[:, TT * b:TT * (b + 1), :], x[:, TT * b:TT * (b + 1), :]).then_inc(stored, 16)
            sp.wait_ge(stored, 16 * NB)

        @block.tensor
        def _(pe):
            def take(step, k=0):
                for reader in sorted((last_reader(*q) for q in before[step][k]), key=lambda r: r[1]):
                    pe.wait_ge(*reader)
                return place(step, k)

            def three(o, w_hi, w_lo, m_hi, m_lo, first, last):
                nc.tensor.matmul(o, w_hi, m_hi, start=first, stop=False)
                nc.tensor.matmul(o, w_hi, m_lo, start=False, stop=False)
                return nc.tensor.matmul(o, w_lo, m_hi, start=False, stop=last)

            def tokens_by_features(o, a_hi, a_lo, base, cols, bias):
                for tt in range(TT):
                    tok = slice(base + tt * P, base + (tt + 1) * P)
                    oo = o[:, tt * D:(tt + 1) * D]
                    for kt in range(KT):
                        last = three(oo, a_hi[:, kt, tok], a_lo[:, kt, tok], wa_hi[:, kt, cols], wa_lo[:, kt, cols],
                                     kt == 0, kt == KT - 1 and bias is None)
                    if bias is not None:
                        last = nc.tensor.matmul(oo, ones_rows[:, :], b_parts[:, bias], start=False, stop=True)
                return last

            for step, l, b, i in order:
                key = (step, l, b, i)
                if step == "QK":
                    if l == 0:
                        pe.wait_ge(wa0_lo, i + 1)
                        pe.wait_ge(xT_done, b + 1)
                    else:
                        pe.wait_ge(w_lo, PREP0 + PREP1)
                        pe.wait_ge(xT_done, NB + nth("XT", 1, b))
                    o = take(key)
                    for j in range(2):
                        c = slice(i * D + j * P, i * D + (j + 1) * P)
                        for kt in range(KT):
                            last = three(o[:, j * T:(j + 1) * T], wa_hi[:, kt, c], wa_lo[:, kt, c],
                                         xT_hi[:, kt, xcols(b)], xT_lo[:, kt, xcols(b)], kt == 0, kt == KT - 1)
                    last.then_inc(qk_mm, 1)
                if step == "V":
                    if l == 0:
                        pe.wait_ge(wa0_lo, 3)
                        pe.wait_ge(xT_done, b + 1)
                    else:
                        pe.wait_ge(w_lo, PREP0 + PREP1)
                        pe.wait_ge(bias_split, 2)
                        pe.wait_ge(bias_moved, 16)
                        pe.wait_ge(xT_done, NB + nth("XT", 1, b))
                    tokens_by_features(take(key), xT_hi, xT_lo, b * T, slice(2 * D, 3 * D),
                                       slice(0, D) if l else None).then_inc(v_mm, 1)
                if step == "S":
                    q, k = q_stack[(b - l) % NB], k_stack[b % 3]
                    if i == 0:
                        pe.wait_ge(q_stacked[(b - l) % NB], 96 * (l + 1))
                        pe.wait_ge(k_stacked[b % 3], 96 * (len(users(l, b)) + 1))
                    for j in range(2):
                        o, h = take(key, j), 2 * i + j
                        nc.tensor.matmul(o[:, 0:T], q[0:KP, h, P:T], k[0:KP, h, :], start=True, stop=True)
                        nc.tensor.matmul(o[:, T:T + P], q[0:KP, h, 0:P], k[0:KP, h, 0:P],
                                         start=True, stop=True).then_inc(s_mm, 1)
                if step == "MX":
                    pe.wait_ge(max_split, nth("MX", l, b))
                    pe.wait_ge(consts, 6)
                    o = take(key)
                    for qt in range(2):
                        last = nc.tensor.matmul(o[0:2 * H, qt * P:(qt + 1) * P], max_hl[:, qt, :, :].rearrange("p c h -> p (c h)"),
                                                ident_b[:, :], start=True, stop=True)
                    last.then_inc(mx_mm, 1)
                if step == "ST":
                    q, k = q_stack[(b - l) % NB], k_stack[b % 3]
                    if i == 0:
                        pe.wait_ge(max_rows, 16 * nth("MX", l, b))
                        pe.wait_ge(minus_rows, 48)
                    o = take(key)
                    for j in range(2):
                        r, h = slice(0, KP + 2), 2 * i + j
                        nc.tensor.matmul(first_keys(o[:, j, 0:T + P]), k[r, h, 0:P],
                                         q[r, h, :].rearrange("p (c t) -> p c t", t=P), start=True, stop=True)
                        last = nc.tensor.matmul(o[:, j, P:T], k[r, h, P:T], q[r, h, P:T],
                                                start=True, stop=True)
                    last.then_inc(st_mm, 1)
                if step == "PV":
                    pe.wait_ge(probs_done, nth("ST", l, b, 2 * i + 1))
                    if i == 0:
                        pe.wait_ge(v_done, nth("V", l, b))
                        pe.wait_ge(v_ones, 3)
                    o = take(key)
                    for kt in range(TT):
                        for g in range(4):
                            s, j = 2 * i + g // 2, g % 2
                            pr = probs[(nth("ST", l, b, s) - 1) % 4]
                            oo, v = o[32 * g:32 * g + 32, kt * P:T], v_aug[b % 3][:, kt, 8 * j + s, :]
                            if kt == 0:
                                last = nc.tensor.matmul(oo.rearrange("p (c t) -> p c t", t=P), v, first_keys(pr[:, j, :]),
                                                        start=True, stop=False)
                            else:
                                last = nc.tensor.matmul(oo, v, pr[:, j, P:T], start=False, stop=True)
                    last.then_inc(pv_mm, 1)
                if step == "UT":
                    pe.wait_ge(u_done, nth("PV", l, b, NGI - 1))
                    for qt in range(TT):
                        o = take(key, qt)
                        for gi in range(NGI):
                            last = nc.tensor.transpose(o[:, gi * P:(gi + 1) * P], u_sb[:, gi, qt * P:(qt + 1) * P],
                                                       ident[:, :])
                        last.then_inc(ut_mm, 1)
                if step == "YT":
                    pe.wait_ge(y_done, 2 * nth("UT", l, b))
                    o = take(key)
                    for kt in range(KT):
                        for tt in range(TT):
                            last = nc.tensor.transpose(o[:, kt * T + tt * P:kt * T + (tt + 1) * P],
                                                       y[:, tt, kt * P:(kt + 1) * P], ident[:, :])
                    last.then_inc(yt_mm, 1)
                if step == "O":
                    pe.wait_ge(yT_done, nth("YT", l, b))
                    if l == 0:
                        pe.wait_ge(wa0_lo, 4)
                    tokens_by_features(take(key), yT_hi, yT_lo, 0, slice(3 * D, 4 * D),
                                       slice(D, 2 * D) if l else None).then_inc(o_mm, 1)
                if step == "XT":
                    pe.wait_ge(ln_done, nth("LN", l, b))
                    o = take(key)
                    for kt in range(KT):
                        for tt in range(TT):
                            last = nc.tensor.transpose(o[:, kt * T + tt * P:kt * T + (tt + 1) * P],
                                                       x[:, TT * b + tt, kt * P:(kt + 1) * P], ident[:, :])
                    last.then_inc(xt_mm, 1)
                if step == "GU":
                    if i == 0:
                        pe.wait_ge(xT_done, NB + nth("XT", 2 * l, b))
                        if b == 0 and l == 0:
                            pe.wait_ge(w_lo, PREP0)
                            pe.wait_ge(w_hi, PREP0)
                        if b == 0 and l == 1:
                            pe.wait_ge(tern_done, 12)
                    o2 = take(key)
                    for part in range(2):
                        for a in range(2):
                            mt = 2 * i + a
                            o = o2[:, part, a * T:(a + 1) * T]
                            for kt in range(KT):
                                x_hi, x_lo = xT_hi[:, kt, xcols(b)], xT_lo[:, kt, xcols(b)]
                                if l == 0:
                                    c = ((kt * 2 + part) * MT0 + mt) * P
                                    last = three(o, gu_hi[:, c:c + P], gu_lo[:, c:c + P], x_hi, x_lo,
                                                 kt == 0, kt == KT - 1)
                                else:
                                    w = (gu_hi, gu_lo)[part]
                                    c = kt * EXPERT + mt * P
                                    nc.tensor.matmul(o, w[:, c:c + P], x_hi, start=(kt == 0), stop=False)
                                    last = nc.tensor.matmul(o, w[:, c:c + P], x_lo, start=False, stop=(kt == KT - 1))
                    last.then_inc(gu_mm, 1)
                if step == "D":
                    nmt = (MT0, MT1)[l]
                    pe.wait_ge(hl_done, nth("HI", l, b, nmt // 2 - 1))
                    o = take(key)
                    for tt in range(TT):
                        tok = slice(tt * P, (tt + 1) * P)
                        oo = o[:, tt * D:(tt + 1) * D]
                        for kt in range(nmt):
                            w = dn[:, kt * D:(kt + 1) * D]
                            h_hi, h_lo = (hidden(l, b, part, kt - kt % 2)[:, kt % 2, tok] for part in range(2))
                            if l == 0:
                                last = three(oo, h_hi, h_lo, w,
                                             dn[:, (MT0 + kt) * D:(MT0 + kt + 1) * D], kt == 0, kt == nmt - 1)
                            else:
                                nc.tensor.matmul(oo, h_hi, w, start=(kt == 0), stop=False)
                                last = nc.tensor.matmul(oo, h_lo, w, start=False, stop=(kt == nmt - 1))
                    last.then_inc(d_mm, 1)
                if step == "TERN" and i % TERN == 1:
                    m = i // TERN
                    pe.wait_ge(abs_done, 4 * (m + 1))
                    nc.tensor.matmul(take(key)[:, 0:4], ones[:, :], abs_sum[:, m, :],
                                     start=True, stop=True).then_inc(sum_mm, 1)

        @block.scalar
        def _(act):
            for step, l, b, i in act_order:
                key = (step, l, b, i)
                if step == "PREPA":
                    c = slice(i * D, (i + 1) * D)
                    act.wait_ge(a0_in[i], 16)
                    nc.scalar.activation(wa_hi[:, :, c], raw_a[:, :, c], ACT.Copy).then_inc(wa0_hi, 1)
                if step == "XPARTS":
                    act.wait_ge(xT_in[b], 16)
                    nc.scalar.activation(xT_hi[:, :, xcols(b)], xT_raw[:, :, xcols(b)], ACT.Copy).then_inc(xT_hi_done, 1)
                if step == "QK":
                    k_ = nth("QK", l, b, i)
                    if k_ > 2:
                        pl, pb = batches[batches.index((l, b)) - 1]
                        if i == 0:
                            act.wait_ge(q_stacked[(pb - pl) % NB], 96 * (pl + 1))
                        else:
                            act.wait_ge(k_stacked[pb % 3], 96 * (len(users(pl, pb)) + 1))
                    if l == 1 and b == 0:
                        act.wait_ge(bias_in, 32)
                    dst = part_of[i][0]
                    act.wait_ge(qk_mm, k_)
                    if l == 0:
                        last = nc.scalar.activation(dst[:, :], place(key)[:, :], ACT.Copy)
                    else:
                        for j in range(2):
                            last = nc.scalar.activation(dst[:, j * T:(j + 1) * T], place(key)[:, j * T:(j + 1) * T],
                                                        ACT.Identity, bias=qk_bias[:, 2 * i + j:2 * i + j + 1])
                    last.then_inc(qk_hi, 1)
                if step == "SPLIT":
                    act.wait_ge(qk_left, nth("SPLIT", l, b, i))
                    nc.scalar.activation(part_of[i][1][:, :], left[i][:, :], ACT.Copy).then_inc(qk_mid, 1)
                if step == "V":
                    act.wait_ge(v_mm, nth("V", l, b))
                    if users(l, b):
                        act.wait_ge(pv_mm, nth("PV", *users(l, b)[-1], NGI - 1))
                    nc.scalar.activation(v_aug[b % 3][:, :, :, 0:HD].rearrange("p t h d -> p (t h) d"),
                                         place(key)[:, :].rearrange("p (th d) -> p th d", d=HD),
                                         ACT.Copy).then_inc(v_done, 1)
                if step == "MX":
                    act.wait_ge(mx_mm, nth("MX", l, b))
                    if nth("MX", l, b) > 1:
                        act.wait_ge(max_rows, 16 * (nth("MX", l, b) - 1))
                    nc.scalar.activation(maxT[:, :], place(key)[0:2 * H, 0:T], ACT.Copy).then_inc(maxT_done, 1)
                if step == "ST":
                    n = nth("ST", l, b, i)
                    act.wait_ge(st_mm, n)
                    if n > 4:
                        _, pl, pb, ps = st_steps[n - 5]
                        act.wait_ge(pv_mm, nth("PV", pl, pb, ps // 2))
                    nc.scalar.activation(probs[(n - 1) % 4][:, :, :], place(key)[:, :, 0:T + P], ACT.Exp,
                                         scale=SC).then_inc(exp_done, 1)
                if step == "PV":
                    act.wait_ge(pv_mm, nth("PV", l, b, i))
                    if i == 0 and (l, b) != (0, 0):
                        act.wait_ge(ut_mm, 2 * nth("UT", *batches[batches.index((l, b)) - 1]))
                    nc.scalar.activation(u_sb[:, i, :], place(key)[:, 0:T], ACT.Copy).then_inc(u_done, 1)
                if step == "YT":
                    act.wait_ge(yt_mm, nth("YT", l, b))
                    nc.scalar.activation(yT_hi[:, :, :], place(key)[:, :].rearrange("p (k t) -> p k t", k=KT),
                                         ACT.Copy).then_inc(yT_hi_done, 1)
                if step == "XT":
                    act.wait_ge(xt_mm, nth("XT", l, b))
                    nc.scalar.activation(xT_hi[:, :, xcols(b)], place(key)[:, :].rearrange("p (k t) -> p k t", k=KT),
                                         ACT.Copy).then_inc(xT_hi_done, 1)
                if step == "GU":
                    n = nth("GU", l, b, i)
                    act.wait_ge(gu_mm, n)
                    if n > 2:
                        act.wait_ge(gated, n - 2)
                    g = place(key)[:, 0, :]
                    if l == 0:
                        if n == 1:
                            act.wait_ge(gains, 2)
                        for a in range(2):
                            mt = 2 * i + a
                            last = nc.scalar.activation(th[n % 2][:, a * T:(a + 1) * T], g[:, a * T:(a + 1) * T],
                                                        ACT.Tanh, scale=half_gs[:, mt:mt + 1])
                    else:
                        last = nc.scalar.activation(th[n % 2][:, :], g, ACT.Tanh, scale=half[:, 0:1])
                    last.then_inc(tanh_done, 1)
                if step == "HI":
                    n = nth("HI", l, b, i)
                    if i == 0 and b < 2:
                        act.wait_ge(st_mm, nth("ST", l, 1 + b, NS - 1))
                    if i == 0 and b >= 2:
                        act.wait_ge(d_mm, nth("D", l, b - 2))
                    act.wait_ge(hf_done, n)
                    nc.scalar.activation(hidden(l, b, 0, 2 * i),
                                         hf[n % 2][:, :].rearrange("p (a t) -> p a t", a=2), ACT.Copy).then_inc(hh_done, 1)
                if step == "PREP0":
                    if i < 4:
                        src, dst = part_of_gate_up(i)
                        act.wait_ge(raw_in, 16 * (i // 2 + 1))
                        nc.scalar.activation(gu_hi[:, dst], raw[:, src], ACT.Copy).then_inc(w_hi, 1)
                    else:
                        k_ = i - 4
                        act.wait_ge(dn_scaled, k_ + 1)
                        nc.scalar.activation(dn[:, k_ * 512:(k_ + 1) * 512], piece[i % 2][:, :], ACT.Copy).then_inc(w_hi, 1)
                if step == "PREP1":
                    c = slice(i * D, (i + 1) * D)
                    act.wait_ge(raw_in, 16 * 4)
                    if i == 0:
                        act.wait_ge(o_mm, nth("O", 0, NB - 1))
                    nc.scalar.activation(wa_hi[:, :, c], raw_a[:, :, c], ACT.Copy).then_inc(w_hi, 1)
                if step == "TERN" and i % TERN == 0:
                    m = i // TERN
                    act.wait_ge(raw_in, 16 * (5 + m))
                    if m == 0:
                        act.wait_ge(gated, nth("GU", 0, NB - 1, MT0 // 2 - 1))
                    for k_ in range(4):
                        if m or k_ > 1:
                            act.wait_ge(abs_done, 4 * m + k_ - 1)
                        nc.scalar.activation(junk[k_ % 2][:, :], raw[:, k_ * 512:(k_ + 1) * 512], ACT.Abs,
                                             accum_out=abs_sum[:, m, k_:k_ + 1]).then_inc(abs_done, 1)

        @block.vector
        def _(dve):
            links = [0]

            def link(ins):
                links[0] += 1
                ins.then_inc(dve_own, 1)
                dve.wait_ge(dve_own, links[0])

            def residual(step, l, b, gain_ap=None):
                n = ln_of(step, l, b)
                k_ = n % 2
                xb = x[:, TT * b:TT * (b + 1), :]
                o = place((step, l, b, 0))[:, :].rearrange("p (t d) -> p t d", t=TT)
                if gain_ap is None:
                    ins = nc.vector.tensor_tensor(res[k_][:, :, :], o, xb, ALU.add)
                else:
                    ins = nc.vector.scalar_tensor_tensor(res[k_][:, :, :], o, gain_ap, xb, ALU.mult, ALU.add)
                ins.then_inc(res_done, 1)
                dve.wait_ge(res_done, n)
                for tt in range(TT):
                    last = nc.vector.bn_stats(stats[k_][:, tt, :], res[k_][:, tt, :])
                link(last)
                for tt in range(TT):
                    last = nc.vector.bn_aggr(mv[k_][:, tt, :], stats[k_][:, tt, :])
                link(last)
                nc.vector.tensor_scalar(mv[k_][:, :, 1], mv[k_][:, :, 1], EPS, None, ALU.add).then_inc(var_done, 1)

            for step, l, b, i in dve_order:
                key = (step, l, b, i)
                if step == "PREPA":
                    c = slice(i * D, (i + 1) * D)
                    dve.wait_ge(wa0_hi, i + 1)
                    nc.vector.tensor_tensor(wa_lo[:, :, c], raw_a[:, :, c], wa_hi[:, :, c].bitcast(fp32),
                                            ALU.subtract).then_inc(wa0_lo, 1)
                if step == "XPARTS":
                    dve.wait_ge(xT_hi_done, b + 1)
                    nc.vector.tensor_tensor(xT_lo[:, :, xcols(b)], xT_raw[:, :, xcols(b)],
                                            xT_hi[:, :, xcols(b)].bitcast(fp32), ALU.subtract).then_inc(xT_done, 1)
                if step == "SCALES":
                    dve.wait_ge(scales_in, 48)
                    nc.vector.tensor_scalar(half_gs[:, :], gs_c[:, :], 0.5, None, ALU.mult).then_inc(gains, 1)
                    dve.wait_ge(gains, 1)
                    nc.vector.tensor_tensor(gain[:, :], half_gs[:, :], us_c[:, :], ALU.mult).then_inc(gains, 1)
                    dve.wait_ge(bias_in, 32)
                    link(nc.vector.tensor_copy(b_parts[0:1, :], b_row[:, :]))
                    dve.wait_ge(consts, 2)
                    nc.vector.tensor_copy(ones_rows[:, :], ones[0:2, :]).then_inc(bias_split, 1)
                    nc.vector.tensor_tensor(b_lo[:, :], b_row[:, :], b_parts[0:1, :].bitcast(fp32),
                                            ALU.subtract).then_inc(bias_split, 1)
                if step == "QK":
                    k_ = nth("QK", l, b, i)
                    dve.wait_ge(qk_hi, k_)
                    if k_ > 2:
                        dve.wait_ge(qk_lo, k_ - 2)
                    src, first = place(key), part_of[i][0]
                    if l == 0:
                        last = nc.vector.tensor_tensor(left[i][:, :], src[:, :], first[:, :], ALU.subtract)
                    else:
                        for j in range(2):
                            c = slice(j * T, (j + 1) * T)
                            last = nc.vector.scalar_tensor_tensor(left[i][:, c], src[:, c], qk_bias[:, 2 * i + j:2 * i + j + 1],
                                                                  first[:, c], ALU.add, ALU.subtract)
                    last.then_inc(qk_left, 1)
                if step == "S":
                    if nth("S", l, b, i) == 1:
                        dve.wait_ge(consts, 6)
                    for j in range(2):
                        n = 2 * nth("S", l, b, i) - 1 + j
                        dve.wait_ge(s_mm, n)
                        if n > 2:
                            dve.wait_ge(max_taken, n - 2)
                        o, h = place(key, j), 2 * i + j
                        nc.vector.tensor_tensor_reduce(out=masked[:, j, 0:T], in0=o[:, 0:T], in1=mask[:, 0:T], scale=1.0,
                                                       scalar=NEG, op0=ALU.add, op1=ALU.max,
                                                       accum_out=row_max[b % 2][:, 1, h:h + 1])
                        nc.vector.tensor_tensor_reduce(out=masked[:, j, T:T + P], in0=o[:, T:T + P], in1=mask[:, T:T + P],
                                                       scale=1.0, scalar=NEG, op0=ALU.add, op1=ALU.max,
                                                       accum_out=row_max[b % 2][:, 0, h:h + 1]).then_inc(max_taken, 1)
                if step == "MX":
                    n = nth("MX", l, b)
                    dve.wait_ge(max_taken, 2 * nth("S", l, b, NS - 1))
                    rm = row_max[b % 2]
                    nc.vector.tensor_copy(max_hl[:, :, 0, :], rm[:, :, :]).then_inc(max_hi, 1)
                    dve.wait_ge(max_hi, n)
                    nc.vector.tensor_tensor(max_hl[:, :, 1, :], rm[:, :, :], max_hl[:, :, 0, :],
                                            ALU.subtract).then_inc(max_split, 1)
                if step == "UT":
                    for qt in range(TT):
                        k_ = 2 * nth("UT", l, b) - 1 + qt
                        dve.wait_ge(ut_mm, k_)
                        o = place(key, qt)[:, :].rearrange("p (s j c) -> p j s c", s=NS, j=2)
                        inv = den_inv[:, qt, :].rearrange("p (j s) -> p j s", j=2)
                        nc.vector.reciprocal(inv, o[:, :, :, HD]).then_inc(inv_done, 1)
                        dve.wait_ge(inv_done, k_)
                        nc.vector.tensor_tensor(y[:, qt, :].rearrange("p (j s d) -> p j s d", j=2, s=NS), o[:, :, :, 0:HD],
                                                inv.unsqueeze(3).broadcast_to([P, 2, NS, HD]), ALU.mult).then_inc(y_done, 1)
                if step == "YT":
                    dve.wait_ge(yT_hi_done, nth("YT", l, b))
                    nc.vector.tensor_tensor(yT_lo[:, :, :], place(key)[:, :].rearrange("p (k t) -> p k t", k=KT),
                                            yT_hi[:, :, :].bitcast(fp32), ALU.subtract).then_inc(yT_done, 1)
                if step == "O":
                    dve.wait_ge(o_mm, nth("O", l, b))
                    if l == 0 and b == 0:
                        dve.wait_ge(x_in, 16)
                    residual("O", l, b)
                if step == "D":
                    dve.wait_ge(d_mm, nth("D", l, b))
                    residual("D", l, b, out_gain[:, 0:1] if l else None)
                if step == "LN":
                    n = nth("LN", l, b)
                    dve.wait_ge(rstd_done, n)
                    for tt in range(TT):
                        ins = nc.vector.tensor_scalar(x[:, TT * b + tt, :], res[n % 2][:, tt, :], mv[n % 2][:, tt, 0:1],
                                                      rstd[n % 2][:, tt:tt + 1], ALU.subtract, ALU.mult)
                    ins.then_inc(ln_done, 1)
                if step == "XT":
                    dve.wait_ge(xT_hi_done, NB + nth("XT", l, b))
                    nc.vector.tensor_tensor(xT_lo[:, :, xcols(b)], place(key)[:, :].rearrange("p (k t) -> p k t", k=KT),
                                            xT_hi[:, :, xcols(b)].bitcast(fp32), ALU.subtract).then_inc(xT_done, 1)
                if step == "GU":
                    n = nth("GU", l, b, i)
                    dve.wait_ge(tanh_done, n)
                    if n > 2:
                        dve.wait_ge(hl_done, n - 2)
                    o = place(key)
                    nc.vector.scalar_tensor_tensor(hf[n % 2][:, :], th[n % 2][:, :], 1.0, o[:, 0, :],
                                                   ALU.add, ALU.mult).then_inc(gated, 1)
                    dve.wait_ge(gated, n)
                    nc.vector.tensor_tensor(hf[n % 2][:, :], hf[n % 2][:, :], o[:, 1, :], ALU.mult).then_inc(hf_done, 1)
                if step == "PREP0" and i >= 4:
                    k_ = i - 4
                    dve.wait_ge(raw_in, 16 * 3)
                    if k_ == 0:
                        dve.wait_ge(gains, 2)
                    if k_ == 2:
                        dve.wait_ge(w_lo, 5)
                    for a in range(2):
                        kt = 2 * k_ + a
                        ins = nc.vector.scalar_tensor_tensor(piece[i % 2][:, a * D:(a + 1) * D], raw[:, kt * D:(kt + 1) * D],
                                                             gain[:, kt:kt + 1], ds_b[:, :], ALU.mult, ALU.mult)
                    ins.then_inc(dn_scaled, 1)
                if step == "TERN" and i % TERN == 1:
                    m = i // TERN
                    c = slice(m, m + 1)
                    dve.wait_ge(sum_mm, m + 1)
                    link(nc.vector.tensor_reduce(total[:, c], place(key)[:, 0:4], mybir.AxisListType.X, ALU.add))
                    link(nc.vector.tensor_scalar(scale[:, c], total[:, c], 1.0 / (D * EXPERT), QEPS, ALU.mult, ALU.add))
                    nc.vector.tensor_scalar(half[:, c], scale[:, c], 0.5, None, ALU.mult)
                    ins = nc.vector.tensor_scalar(minus[:, c], scale[:, c], -0.5, None, ALU.mult)
                    if m == 2:
                        link(nc.vector.tensor_tensor(out_gain[:, :], half[:, 0:1], scale[:, 1:2], ALU.mult))
                        ins = nc.vector.tensor_tensor(out_gain[:, :], out_gain[:, :], scale[:, 2:3], ALU.mult)
                    ins.then_inc(thresholds, 1)
                if step == "TERN" and i % TERN >= 2:
                    m, c, dst = ternary_piece(i)
                    n = 4 * m + i % TERN - 1
                    dve.wait_ge(below, n)
                    nc.vector.scalar_tensor_tensor(dst, raw[:, c], half[:, m:m + 1], piece[n % 2][:, :],
                                                   ALU.is_gt, ALU.subtract).then_inc(tern_done, 1)

        @block.gpsimd
        def _(pool):
            pool.memset(minus_ones[:, :], -1.0).then_inc(consts, 1)
            pool.memset(ones[:, :], 1.0).then_inc(consts, 1)
            pool.memset(ident_b[:, :], 0.0).then_inc(pool_own, 1)
            pool.memset(minus_half[:, :], -0.5)
            pool.memset(ident[:, :], 0.0).then_inc(pool_own, 1)
            pool.memset(mask[:, :], 0.0).then_inc(pool_own, 1)
            pool.wait_ge(pool_own, 3)
            pool.affine_select(out=ident_b[:, :], in_=ident_b[:, :], compare_op=ALU.not_equal, fill=1.0, base=0,
                               pattern=[[-1, P]], channel_multiplier=1).then_inc(consts, 1)
            pool.affine_select(out=ident[:, :], in_=ident[:, :], compare_op=ALU.not_equal, fill=1.0, base=0,
                               pattern=[[-1, P]], channel_multiplier=1).then_inc(consts, 1)
            pool.affine_select(out=mask[:, 0:T], in_=mask[:, 0:T], compare_op=ALU.is_ge, fill=NEG, base=P,
                               pattern=[[-1, T]], channel_multiplier=1).then_inc(consts, 1)
            pool.affine_select(out=mask[:, T:T + P], in_=mask[:, T:T + P], compare_op=ALU.is_ge, fill=NEG, base=0,
                               pattern=[[-1, P]], channel_multiplier=1).then_inc(consts, 1)
            for n in range(3):
                pool.memset(v_aug[n][:, :, :, HD:2 * HD], 1.0).then_inc(v_ones, 1)

            for step, l, b, i in pool_order:
                if step == "SPLIT":
                    pool.wait_ge(qk_mid, nth("SPLIT", l, b, i))
                    pool.tensor_tensor(part_of[i][2][:, :], left[i][:, :], part_of[i][1][:, :],
                                       ALU.subtract).then_inc(qk_lo, 1)
                if step == "ST":
                    n = nth("ST", l, b, i)
                    pool.wait_ge(exp_done, n)
                    diag = probs[(n - 1) % 4][:, :, 0:T]
                    pool.affine_select(out=diag, in_=diag, compare_op=ALU.is_ge, fill=0.0, base=0,
                                       pattern=[[0, 2], [0, 2], [1, P]], channel_multiplier=-1).then_inc(probs_done, 1)
                if step == "LN":
                    n = nth("LN", l, b)
                    pool.wait_ge(var_done, n)
                    pool.tensor_tensor(rstd[n % 2][:, :], mv[n % 2][:, :, 1], minus_half[:, :], ALU.pow).then_inc(rstd_done, 1)
                if step == "HI":
                    n = nth("HI", l, b, i)
                    pool.wait_ge(hh_done, n)
                    pool.tensor_tensor(hidden(l, b, 1, 2 * i), hf[n % 2][:, :].rearrange("p (a t) -> p a t", a=2),
                                       hidden(l, b, 0, 2 * i).bitcast(fp32), ALU.subtract).then_inc(hl_done, 1)
                if step == "PREP0":
                    pool.wait_ge(w_hi, i + 1)
                    if i < 4:
                        src, dst = part_of_gate_up(i)
                        last = pool.tensor_tensor(gu_lo[:, dst], raw[:, src], gu_hi[:, dst].bitcast(fp32), ALU.subtract)
                    else:
                        k_ = i - 4
                        last = pool.tensor_tensor(dn[:, MT0 * D + k_ * 512:MT0 * D + (k_ + 1) * 512], piece[i % 2][:, :],
                                                  dn[:, k_ * 512:(k_ + 1) * 512].bitcast(fp32), ALU.subtract)
                    last.then_inc(w_lo, 1)
                if step == "PREP1":
                    c = slice(i * D, (i + 1) * D)
                    pool.wait_ge(w_hi, PREP0 + i + 1)
                    pool.tensor_tensor(wa_lo[:, :, c], raw_a[:, :, c], wa_hi[:, :, c].bitcast(fp32),
                                       ALU.subtract).then_inc(w_lo, 1)
                if step == "TERN" and i % TERN >= 2:
                    m, c, _ = ternary_piece(i)
                    n = 4 * m + i % TERN - 1
                    pool.wait_ge(thresholds, m + 1)
                    if n > 2:
                        pool.wait_ge(tern_done, n - 2)
                    pool.tensor_scalar(piece[n % 2][:, :], raw[:, c], minus[:, m:m + 1], None, ALU.is_lt).then_inc(below, 1)


_OUT = (NB, T, D)


def kernel(**inputs):
    import numpy as np
    import concourse.bacc as bacc
    from concourse.bass_utils import run_bass_kernel_spmd

    a = {k: np.asarray(v) for k, v in inputs.items()}

    def k_major(w):
        n, k = w.shape
        return np.ascontiguousarray(w.T.reshape(k // P, P, n).transpose(1, 0, 2))

    def by_stack(w):
        return w.reshape((2, NS, HD) + w.shape[1:]).swapaxes(1, 2).reshape(w.shape)

    def attention_weights(q, k, v, o):
        return np.concatenate([k_major(by_stack(q)), k_major(by_stack(k)), k_major(v), k_major(o)], axis=2)

    def by_partition(w, tiles):
        padded = np.zeros((tiles * P,) + w.shape[1:], w.dtype)
        padded[:w.shape[0]] = w
        return np.ascontiguousarray(padded.reshape((tiles, P) + w.shape[1:]).swapaxes(0, 1))

    wp = a["L0_attn_w_project"]
    gate_up = np.zeros((P, KT, 2, MT0 * P), np.float32)
    gate_up[..., 0, :INTER] = k_major(a["L0_ffn_gate_w"])
    gate_up[..., 1, :INTER] = k_major(a["L0_ffn_up_w"])
    tokens = a["L0_attn_x"].reshape(NB * T, D)
    bias = np.stack([by_stack(a["L1_attn_bq"]).reshape(2, P), by_stack(a["L1_attn_bk"]).reshape(2, P)])
    arrays = {
        "x_nat": tokens.reshape(NB * TT, P, D).transpose(1, 0, 2),
        "x_tr": k_major(tokens),
        "a0": attention_weights(wp[:D], wp[D:2 * D], wp[2 * D:], a["L0_attn_w_out"]),
        "f0gu": gate_up.reshape(P, KT, 2 * MT0 * P),
        "f0dn": by_partition(a["L0_ffn_down_w"].T, MT0).reshape(P, MT0 * D),
        "gs": by_partition(a["L0_ffn_gate_s"], MT0),
        "us": by_partition(a["L0_ffn_up_s"], MT0),
        "ds": a["L0_ffn_down_s"],
        "a1": attention_weights(a["L1_attn_Wq"], a["L1_attn_Wk"], a["L1_attn_Wv"], a["L1_attn_Wo"]).reshape(P, 4 * KT * D),
        "bqk": bias.reshape(4, P).T,
        "brow": np.concatenate([a["L1_attn_bv"], a["L1_attn_bo"]]).reshape(1, 2 * D),
        "f1": np.stack([k_major(a["L1_ffn_W_up"]).reshape(P, -1), k_major(a["L1_ffn_W_gate"]).reshape(P, -1),
                        k_major(a["L1_ffn_W_down"]).reshape(P, -1)], axis=1),
    }
    arrays = {k: np.ascontiguousarray(v) for k, v in arrays.items()}
    nc = bacc.Bacc("TRN2", target_bir_lowering=False, num_devices=1)
    aps = [nc.dram_tensor(k, v.shape, fp32, kind="ExternalInput").ap() for k, v in arrays.items()]
    out = nc.dram_tensor("out", (P, NB * TT, D), fp32, kind="ExternalOutput").ap()
    program(nc, *aps, out)
    r = run_bass_kernel_spmd(nc, [arrays], core_ids=[0])
    y = r.results[0]["out"]
    return np.ascontiguousarray(y.transpose(1, 0, 2)).reshape(_OUT)
```
